# Optimizing a Trainium2 kernel written in Bass

```python
import numpy as np
import jax
import jax.numpy as jnp

def _softmax(x, axis=-1):
    return jax.nn.softmax(x, axis=axis)

def _gelu(x):
    return jax.nn.gelu(x, approximate=True)

def _silu(x):
    return jax.nn.silu(x)

def _sigmoid(x):
    return jax.nn.sigmoid(x)

def _layernorm(x, axis=-1, eps=1e-05):
    m = jnp.mean(x, axis=axis, keepdims=True)
    v = jnp.var(x, axis=axis, keepdims=True)
    return (x - m) / jnp.sqrt(v + eps)

def _scatter_add(tgt, idx, src, axis=0):
    return tgt.at[idx].add(src)

def _segment_sum(src, seg, n):
    return jax.ops.segment_sum(src, seg, n)
kernel_name = 'mk_decoder_postln_d1_seqx_r8_769399'

def setup_inputs(seed: int=0):
    np.random.seed(seed)
    _w = jnp.asarray

    def _rec_inputs():
        import jax
        import jax.numpy as jnp
        _rk = jax.random.key(seed)
        x = -0.0002928 + 1 * jax.random.normal(jax.random.fold_in(_rk, 1), (128, 64, 128), jnp.float32)
        _lenS = 64 - jax.random.randint(jax.random.fold_in(_rk, 7), (128,), 0, max(1, 64 // 4) + 1, jnp.int32)
        _lenS2 = 64 - jax.random.randint(jax.random.fold_in(_rk, 8), (128,), 0, max(1, 64 // 4) + 1, jnp.int32)
        _ctx_1024P = jax.random.normal(jax.random.fold_in(_rk, 11), (128, 16, 128), jnp.float32)
        _ctx_1024c = jax.random.dirichlet(jax.random.fold_in(_rk, 511), 0.3 * jnp.ones((16,), jnp.float32), (128, 64))
        _ctx_1024t = jnp.einsum('bsk,bkd->bsd', _ctx_1024c, _ctx_1024P)
        _ctx_1024t = _ctx_1024t * jax.lax.rsqrt(jnp.mean(jnp.square(_ctx_1024t)) + 1e-12) * 0.953939
        ctx_1024 = -1.39393e-06 + 0.999914 * (_ctx_1024t + 0.3 * jax.random.normal(jax.random.fold_in(_rk, 611), (128, 64, 128), jnp.float32))
        return (x, ctx_1024)
    x, ctx_1024 = _rec_inputs()

    def _L0_attn_setup():
        import jax, jax.numpy as jnp
        import numpy as np
        B, N, DIM = (2, 512, 128)
        H, DH, F = (16, 64, 32)
        key = jax.random.key(seed)
        ks = jax.random.split(key, 12)
        s = 1.0 / np.sqrt(DIM)
        inp = {'x': jax.random.normal(ks[0], (B, N, DIM), jnp.float32), 'Wq': jax.random.normal(ks[1], (DIM, H * DH), jnp.float32) * s, 'bq': jax.random.normal(ks[2], (H * DH,), jnp.float32) * 0.02, 'Wk': jax.random.normal(ks[3], (DIM, H * DH), jnp.float32) * s, 'bk': jax.random.normal(ks[4], (H * DH,), jnp.float32) * 0.02, 'Wv': jax.random.normal(ks[5], (DIM, H * DH), jnp.float32) * s, 'bv': jax.random.normal(ks[6], (H * DH,), jnp.float32) * 0.02, 'Wproj': jax.random.normal(ks[7], (H * DH, DIM), jnp.float32) * s, 'bproj': jax.random.normal(ks[8], (DIM,), jnp.float32) * 0.02, 'wq_feat': jax.random.normal(ks[9], (DH, F), jnp.float32) / np.sqrt(DH), 'wk_feat': jax.random.normal(ks[10], (DH, F), jnp.float32) / np.sqrt(DH)}
        return inp
    _L0_attn_all = _L0_attn_setup()
    _L0_attn_in = {k: v for k, v in _L0_attn_all.items() if k in ('Wq', 'bq', 'Wk', 'bk', 'Wv', 'bv', 'Wproj', 'bproj', 'wq_feat', 'wk_feat')}
    del _L0_attn_all

    def _L0_xattn_setup():
        import jax, jax.numpy as jnp
        import numpy as np
        HIDDEN = 128
        HEADS = 16
        HEAD_DIM = HIDDEN // HEADS
        key = jax.random.key(seed)
        ks = jax.random.split(key, 12)
        B, S, D = (2, 256, HIDDEN)
        scale = 1.0 / np.sqrt(D)
        return {'query': jax.random.normal(ks[0], (B, S, D), jnp.float32), 'key': jax.random.normal(ks[1], (B, S, D), jnp.float32), 'value': jax.random.normal(ks[2], (B, S, D), jnp.float32), 'Wq': jax.random.normal(ks[3], (D, D), jnp.float32) * scale, 'bq': jnp.zeros((D,), jnp.float32), 'Wk': jax.random.normal(ks[4], (D, D), jnp.float32) * scale, 'bk': jnp.zeros((D,), jnp.float32), 'Wv': jax.random.normal(ks[5], (D, D), jnp.float32) * scale, 'bv': jnp.zeros((D,), jnp.float32), 'Wo': jax.random.normal(ks[6], (D, D), jnp.float32) * scale, 'bo': jnp.zeros((D,), jnp.float32)}
    _L0_xattn_all = _L0_xattn_setup()
    _L0_xattn_in = {k: v for k, v in _L0_xattn_all.items() if k in ('Wq', 'bq', 'Wk', 'bk', 'Wv', 'bv', 'Wo', 'bo')}
    del _L0_xattn_all

    def _L0_ffn_setup():
        import jax, jax.numpy as jnp
        import numpy as np
        EPS = 1e-06
        LN_EPS = 1e-05

        def _absmean_core(W):
            gamma = jnp.mean(jnp.abs(W)) + EPS
            Ws = W / gamma
            Wq = jnp.sign(Ws) * jnp.minimum(jnp.round(jnp.abs(Ws)), 1.0)
            return (Wq, gamma)

        @jax.custom_vjp
        def absmean(W):
            return _absmean_core(W)[0]

        def _absmean_fwd(W):
            Wq, gamma = _absmean_core(W)
            return (Wq, gamma)

        def _absmean_bwd(gamma, g):
            return (g / gamma,)
        absmean.defvjp(_absmean_fwd, _absmean_bwd)

        def layernorm(x, w, b, eps=LN_EPS):
            mu = jnp.mean(x, axis=-1, keepdims=True)
            var = jnp.mean((x - mu) ** 2, axis=-1, keepdims=True)
            return (x - mu) * jax.lax.rsqrt(var + eps) * w + b
        key = jax.random.key(seed)
        k1, k2, k3 = jax.random.split(key, 3)
        d, h = (128, 512)
        B, T = (8, 256)
        return {'x': jax.random.normal(k1, (B, T, d), jnp.float32), 'W_fc': jax.random.normal(k2, (h, d), jnp.float32), 'ln_w': jnp.ones((h,), jnp.float32), 'ln_b': jnp.zeros((h,), jnp.float32), 'W_proj': jax.random.normal(k3, (d, h), jnp.float32)}
    _L0_ffn_all = _L0_ffn_setup()
    _L0_ffn_in = {k: v for k, v in _L0_ffn_all.items() if k in ('W_fc', 'ln_w', 'ln_b', 'W_proj')}
    del _L0_ffn_all
    return {'x': x, 'ctx_1024': ctx_1024, 'L0_attn_Wq': _L0_attn_in['Wq'], 'L0_attn_bq': _L0_attn_in['bq'], 'L0_attn_Wk': _L0_attn_in['Wk'], 'L0_attn_bk': _L0_attn_in['bk'], 'L0_attn_Wv': _L0_attn_in['Wv'], 'L0_attn_bv': _L0_attn_in['bv'], 'L0_attn_Wproj': _L0_attn_in['Wproj'], 'L0_attn_bproj': _L0_attn_in['bproj'], 'L0_attn_wq_feat': _L0_attn_in['wq_feat'], 'L0_attn_wk_feat': _L0_attn_in['wk_feat'], 'L0_xattn_Wq': _L0_xattn_in['Wq'], 'L0_xattn_bq': _L0_xattn_in['bq'], 'L0_xattn_Wk': _L0_xattn_in['Wk'], 'L0_xattn_bk': _L0_xattn_in['bk'], 'L0_xattn_Wv': _L0_xattn_in['Wv'], 'L0_xattn_bv': _L0_xattn_in['bv'], 'L0_xattn_Wo': _L0_xattn_in['Wo'], 'L0_xattn_bo': _L0_xattn_in['bo'], 'L0_ffn_W_fc': _L0_ffn_in['W_fc'], 'L0_ffn_ln_w': _L0_ffn_in['ln_w'], 'L0_ffn_ln_b': _L0_ffn_in['ln_b'], 'L0_ffn_W_proj': _L0_ffn_in['W_proj']}

def reference(x, ctx_1024, L0_attn_Wq, L0_attn_bq, L0_attn_Wk, L0_attn_bk, L0_attn_Wv, L0_attn_bv, L0_attn_Wproj, L0_attn_bproj, L0_attn_wq_feat, L0_attn_wk_feat, L0_xattn_Wq, L0_xattn_bq, L0_xattn_Wk, L0_xattn_bk, L0_xattn_Wv, L0_xattn_bv, L0_xattn_Wo, L0_xattn_bo, L0_ffn_W_fc, L0_ffn_ln_w, L0_ffn_ln_b, L0_ffn_W_proj):
    import jax
    import jax.numpy as jnp

    def _L0_attn_ref(x, Wq, bq, Wk, bk, Wv, bv, Wproj, bproj, wq_feat, wk_feat):
        import jax, jax.numpy as jnp
        import numpy as np
        B, N, DIM = (2, 512, 128)
        H, DH, F = (16, 64, 32)
        b, n, _ = x.shape
        q = (x @ Wq + bq).reshape(b, n, H, DH)
        k = (x @ Wk + bk).reshape(b, n, H, DH)
        v = (x @ Wv + bv).reshape(b, n, H, DH)
        q_prime = jnp.exp(jnp.einsum('bnhd,df->bnhf', q, wq_feat))
        k_prime = jnp.exp(jnp.einsum('bnhd,df->bnhf', k, wk_feat))
        k_sum = k_prime.sum(axis=1)
        D_inv = 1.0 / (jnp.einsum('bnhf,bhf->bnh', q_prime, k_sum) + 1e-06)
        context = jnp.einsum('bnhf,bnhd->bhfd', k_prime, v)
        out = jnp.einsum('bnhf,bhfd,bnh->bnhd', q_prime, context, D_inv)
        out = out.reshape(b, n, H * DH)
        return out @ Wproj + bproj

    def _L0_xattn_ref(query, key, value, Wq, bq, Wk, bk, Wv, bv, Wo, bo):
        import jax, jax.numpy as jnp
        import numpy as np
        HIDDEN = 128
        HEADS = 16
        HEAD_DIM = HIDDEN // HEADS
        B, S, D = query.shape
        H, Hd = (HEADS, HEAD_DIM)
        sm_scale = 1.0 / jnp.sqrt(jnp.asarray(Hd, query.dtype))

        def proj(x, W, b):
            y = jnp.einsum('bsd,ed->bse', x, W) + b
            return y.reshape(B, S, H, Hd).transpose(0, 2, 1, 3)
        Q = proj(query, Wq, bq)
        K = proj(key, Wk, bk)
        V = proj(value, Wv, bv)
        scores = jnp.einsum('bhqd,bhkd->bhqk', Q, K) * sm_scale
        attn = jax.nn.softmax(scores, axis=-1)
        ctx = jnp.einsum('bhqk,bhkd->bhqd', attn, V)
        ctx = ctx.transpose(0, 2, 1, 3).reshape(B, S, D)
        out = jnp.einsum('bsd,ed->bse', ctx, Wo) + bo
        return out

    def _L0_ffn_ref(x, W_fc, ln_w, ln_b, W_proj):
        import jax, jax.numpy as jnp
        import numpy as np
        EPS = 1e-06
        LN_EPS = 1e-05

        def _absmean_core(W):
            gamma = jnp.mean(jnp.abs(W)) + EPS
            Ws = W / gamma
            Wq = jnp.sign(Ws) * jnp.minimum(jnp.round(jnp.abs(Ws)), 1.0)
            return (Wq, gamma)

        @jax.custom_vjp
        def absmean(W):
            return _absmean_core(W)[0]

        def _absmean_fwd(W):
            Wq, gamma = _absmean_core(W)
            return (Wq, gamma)

        def _absmean_bwd(gamma, g):
            return (g / gamma,)
        absmean.defvjp(_absmean_fwd, _absmean_bwd)

        def layernorm(x, w, b, eps=LN_EPS):
            mu = jnp.mean(x, axis=-1, keepdims=True)
            var = jnp.mean((x - mu) ** 2, axis=-1, keepdims=True)
            return (x - mu) * jax.lax.rsqrt(var + eps) * w + b
        h = jnp.einsum('btd,hd->bth', x, absmean(W_fc))
        h = jax.nn.gelu(h, approximate=False)
        h = layernorm(h, ln_w, ln_b)
        return jnp.einsum('bth,dh->btd', h, absmean(W_proj))
    x = _layernorm(x + _L0_attn_ref(x, L0_attn_Wq, L0_attn_bq, L0_attn_Wk, L0_attn_bk, L0_attn_Wv, L0_attn_bv, L0_attn_Wproj, L0_attn_bproj, L0_attn_wq_feat, L0_attn_wk_feat), axis=-1)
    x = _layernorm(x + _L0_xattn_ref(x, ctx_1024, ctx_1024, L0_xattn_Wq, L0_xattn_bq, L0_xattn_Wk, L0_xattn_bk, L0_xattn_Wv, L0_xattn_bv, L0_xattn_Wo, L0_xattn_bo), axis=-1)
    x = _layernorm(x + _L0_ffn_ref(x, L0_ffn_W_fc, L0_ffn_ln_w, L0_ffn_ln_b, L0_ffn_W_proj), axis=-1)
    return x

_drawn_inputs = setup_inputs


def setup_inputs(seed=0):
    import zlib

    import numpy as np

    out = dict(_drawn_inputs(seed))
    spreads = {'L0_xattn_bq': (0.0, 0.291),
     'L0_xattn_bk': (0.0, 2.0),
     'L0_xattn_bv': (0.0, 0.1),
     'L0_xattn_bo': (0.0, 0.1),
     'L0_ffn_ln_w': (1.0, 0.2),
     'L0_ffn_ln_b': (0.0, 0.1)}
    factors = {'L0_attn_bq': 23.123, 'L0_attn_bk': 8.0, 'L0_attn_bproj': 2.677}
    for name, (base, spread) in spreads.items():
        noise = np.random.default_rng([zlib.crc32(name.encode()), seed]).standard_normal(out[name].shape)
        drawn = base * np.exp(spread * noise) if base else spread * noise
        out[name] = jnp.asarray(drawn.astype(out[name].dtype))
    for name, factor in factors.items():
        out[name] = (out[name] * factor).astype(out[name].dtype)
    return out
```

```python
import numpy as np
import concourse.bass as bass
from concourse import mybir
from contextlib import ExitStack

NB = 128
T = 64
D = 128
NG = 16
H = 16


class Queues:

    def __init__(self, nc, ctx):
        self.nc, self.ctx = nc, ctx
        self.sems, self.count = {}, {}
        self.lists = {e: [] for e in ("pe", "act", "dve", "pool", "sp")}

    def add(self, eng, fn, waits=(), sig=None, inc=1):
        done = None
        if sig is not None:
            if sig not in self.sems:
                self.sems[sig] = self.ctx.enter_context(self.nc.semaphore("s_" + sig))
                self.count[sig] = 0
            self.count[sig] += inc
            done = (sig, self.count[sig])
        self.lists[eng].append((fn, tuple(w for w in waits if w is not None), sig, inc))
        return done

    def emit(self, eng, e):
        seen = {}
        for fn, waits, sig, inc in self.lists[eng]:
            need = {}
            for name, value in waits:
                need[name] = max(need.get(name, 0), value)
            for name, value in need.items():
                if seen.get(name, 0) < value:
                    e.wait_ge(self.sems[name], value)
                    seen[name] = value
            ins = fn(e)
            if sig is not None:
                ins.then_inc(self.sems[sig], inc)


class Banks:

    def __init__(self, banks):
        self.banks, self.freed, self.n = banks, [()] * len(banks), 0

    def get(self):
        i = self.n % len(self.banks)
        self.n += 1
        return i, self.banks[i], self.freed[i]

    def free(self, i, *reads):
        self.freed[i] = reads


def decoder_kernel(nc, a, out):
    F32, F16, BF = mybir.dt.float32, mybir.dt.float16, mybir.dt.bfloat16
    ALU, ACT, AX = mybir.AluOpType, mybir.ActivationFunctionType, mybir.AxisListType
    SM = 8.0 ** -0.5

    with ExitStack() as ctx:
        q = Queues(nc, ctx)
        add = q.add

        def sb(name, cols, dt=F32, parts=128):
            return ctx.enter_context(nc.sbuf_tensor(name, [parts, cols], dt))

        banks = [ctx.enter_context(nc.psum_tensor(f"bank{i}", [128, 512], F32)) for i in range(8)]
        PA, PB, PC = Banks(banks[0:3]), Banks(banks[3:6]), Banks(banks[6:8])

        held = {}

        def load(name, dt=F32, t=None):
            shape = a[name].shape
            if t is None:
                t = sb("w_" + name, shape[1], dt, shape[0])
            add("sp", lambda e, t=t, n=name: e.dma_start(t[:, :], a[n]), sig="weights", inc=16)
            held[name] = t
            return t

        two = range(2)
        Qblk, PT = sb("Qblk", 8192, F16), [sb(f"PT{i}", 1024) for i in two]
        WqT, WkT, WvT, Wpj = [load(n, t=Qblk[:, 2048 * i:2048 * i + 2048].bitcast(F32)) for i, n in enumerate(("WqT", "WkT", "WvT", "Wpj"))]
        bvblk, bvrep = load("bvblk", t=PT[0]), load("bvrep", t=PT[1])
        fq, fk = load("featq"), load("featk")
        bqT, bkT = load("bqT"), load("bkT")
        bpj, bo = load("bproj"), load("bo")
        xWq, xWk = load("xWq"), load("xWk")
        xbq, xbk, xbql, xbkl = load("xbq"), load("xbk"), load("xbql"), load("xbkl")
        xWv, xWo, xbv = load("xWv"), load("xWo"), load("xbvrep")
        Wfc, Wpr = load("Wfc"), load("Wpr")
        lnw, lnb = load("lnw"), load("lnbrep")
        ident, hmask, dmask = load("ident"), load("hmask"), load("dmask")
        onesblk, lowq, lowk, jm = load("onesblk"), load("lowq"), load("lowk"), load("jm")
        kp, sel = sb("kp", 2048), sb("sel", 2048, BF)
        selw = load("sel", t=kp)
        jmask2 = load("jmask2")
        n_w = len(held)
        weights = ("weights", 16 * n_w)

        ones = sb("ones", 128)
        mhalf = sb("mhalf", 4)
        o1 = add("dve", lambda e: e.memset(ones[:, :], 1.0), sig="const")
        o2 = add("dve", lambda e: e.memset(mhalf[:, :], -0.5), sig="const")

        Wqf, Wkf, Mh = sb("Wqf", 512), sb("Wkf", 512), sb("Mh", 2048)
        qb = sb("qb", 4)
        nbeta, biasA, bias2, bias3 = sb("nbeta", 128), sb("biasA", 128), sb("bias2", 128), sb("bias3", 128)
        tfc, tpr, Aw = sb("tfc", 512, F16), sb("tpr", 512), sb("Aw", 512)

        def prep():
            def pe(fns, waits, sig="w_pe"):
                for f in fns[:-1]:
                    add("pe", f, waits)
                    waits = ()
                return add("pe", fns[-1], waits, sig=sig)

            ready = [add("dve", lambda e: e.tensor_copy(sel[:, :], selw[:, :]), [weights], sig="w_dve")]
            for W, f, dst in ((WqT, fq, Wqf), (WkT, fk, Wkf)):
                i, bk, fr = PA.get()
                m = pe([lambda e, W=W, f=f, bk=bk, c=c: e.matmul(bk[:, c * 64:c * 64 + 64], W[:, c * 128:c * 128 + 128], f[:, :], start=True, stop=True)
                        for c in range(8)], [weights, *fr])
                r = add("act", lambda e, bk=bk, dst=dst: e.activation(dst[:, :], bk[:, :], ACT.Copy), [m], sig="w_act")
                PA.free(i, r)
                ready.append(r)
            i, bk, fr = PA.get()
            fns = []
            for hp in range(2):
                o = bk[64 * hp:64 * hp + 64, 0:4]
                fns.append(lambda e, o=o, hp=hp: e.matmul(o, fq[:, :], bqT[:, hp::2], start=True, stop=False))
                fns.append(lambda e, o=o, hp=hp: e.matmul(o, fk[:, :], bkT[:, hp::2], start=False, stop=True))
            m = pe(fns, fr)
            r = add("act", lambda e, bk=bk: e.activation(qb[:, :], bk[:, 0:4], ACT.Copy), [m], sig="w_act")
            PA.free(i, r)
            ready.append(r)
            for c in range(4):
                i, bk, fr = PA.get()
                fns = []
                hp, r0 = c % 2, 64 * (c % 2)
                for k in range(4):
                    w = slice((4 * (c // 2) + k) * 128, (4 * (c // 2) + k) * 128 + 128)
                    fns.append(lambda e, bk=bk, k=k, w=w, r0=r0: e.matmul(
                        bk[:, k * 128:k * 128 + 128], WvT[r0:r0 + 64, w], Wpj[r0:r0 + 64, w], start=True, stop=True))
                m = pe(fns, fr)
                o = Mh[:, :].rearrange("p (c k a n) -> p c k a n", c=2, k=4, a=2)[:, c // 2, :, hp, :]
                r = add("act", lambda e, bk=bk, o=o: e.activation(o, bk[:, :].rearrange("p (k n) -> p k n", k=4), ACT.Copy), [m], sig="w_act")
                PA.free(i, r)
                ready.append(r)

            def acc(lhs, rhs, row, n):
                fns = [lambda e, c=c, bk=bk: e.matmul(bk[:, 0:128], lhs[:, c * 128:c * 128 + 128], rhs[:, c * 128:c * 128 + 128],
                                                      start=(c == 0), stop=(c == n - 1 and row is None)) for c in range(n)]
                if row is not None:
                    fns.append(lambda e, bk=bk: e.matmul(bk[:, 0:128], ones[0:1, 0:128], row[0:1, :], start=False, stop=True))
                return fns

            for lhs, rhs, row, n, dst, scale in ((bvblk, Wpj, None, 8, nbeta, -1e-6), (bvrep, Wpj, bpj, 8, biasA, 1.0),
                                                 (xbv, xWo, bo, 1, bias2, 1.0)):
                i, bk, fr = PA.get()
                m = pe(acc(lhs, rhs, row, n), [o1, *fr])
                r = add("act", lambda e, bk=bk, dst=dst, scale=scale: e.activation(dst[:, :], bk[:, 0:128], ACT.Copy, scale=scale), [m], sig="w_act")
                PA.free(i, r)
                ready.append(r)
            colsum, hg, tmp = sb("colsum", 2), sb("hg", 4), sb("tmp", 512)
            for n, W in enumerate((Wfc, Wpr)):
                c = add("dve", lambda e, n=n, W=W: e.tensor_reduce(colsum[:, n:n + 1], W[:, :], AX.X, ALU.add, apply_absolute_value=True),
                        [weights], sig="w_dve")
            i, bk, fr = PA.get()
            m = pe([lambda e, bk=bk: e.matmul(bk[:, 0:2], ones[:, :], colsum[:, :], start=True, stop=True)], [c, *fr])
            h1 = add("dve", lambda e, bk=bk: e.tensor_scalar(hg[:, 0:2], bk[:, 0:2], 1.0 / 65536, 1e-6, ALU.mult, ALU.add), [m], sig="w_dve")
            PA.free(i, h1)
            h2 = add("dve", lambda e: e.tensor_scalar(hg[:, 2:4], hg[:, 0:2], -0.5, None, ALU.mult), [h1], sig="w_dve")
            h3 = add("dve", lambda e: e.tensor_scalar(hg[:, 0:2], hg[:, 0:2], 0.5, None, ALU.mult), [h2], sig="w_dve")
            for n, (W, dst) in enumerate(((Wfc, tfc), (Wpr, tpr))):
                t1 = add("dve", lambda e, n=n, W=W: e.tensor_scalar(tmp[:, :], W[:, :], hg[:, 2 + n:3 + n], None, ALU.is_lt), [h3], sig="w_dve")
                h3 = add("dve", lambda e, n=n, W=W, dst=dst: e.scalar_tensor_tensor(dst[:, :], W[:, :], hg[:, n:n + 1], tmp[:, :], ALU.is_gt, ALU.subtract),
                         [t1], sig="w_dve")
            for c in range(4):
                h4 = add("dve", lambda e, c=c: e.tensor_scalar(Aw[:, c * 128:c * 128 + 128], tpr[:, c * 128:c * 128 + 128], lnw[:, c:c + 1], None, ALU.mult),
                         [h3], sig="w_dve")
            ready.append(h4)
            i, bk, fr = PA.get()
            m = pe(acc(lnb, tpr, None, 4), [h3, *fr])
            r = add("act", lambda e, bk=bk: e.activation(bias3[:, :], bk[:, 0:128], ACT.Copy), [m], sig="w_act")
            PA.free(i, r)
            ready.append(r)
            return ready

        prepared = prep()

        xs, xT, cxT = [sb(f"xs{i}", 512) for i in two], [sb(f"xT{i}", 512) for i in two], [sb(f"cxT{i}", 512) for i in two]
        qT = [sb(f"qT{i}", 2048) for i in two]
        kblkT, kblk, Dn, xb = sb("kblkT", 512), sb("kblk", 512), sb("Dn", 512), sb("xb", 512)
        GT, Cb = [sb(f"GT{i}", 512) for i in range(3)], [sb(f"Cb{i}", 512) for i in range(4)]
        r1, x1, x1b, x1T = sb("r1", 512), sb("x1", 512), [sb(f"x1b{i}", 512) for i in two], [sb(f"x1T{i}", 512) for i in two]
        Qh, Qs = [sb(f"Qh{i}", 512, F16) for i in two], [sb(f"Qs{i}", 512, F16) for i in two]
        Ks = sb("Ks", 2048, F16)
        Vblk = sb("Vblk", 2048)
        mx, Mrow = sb("mx", 64), sb("Mrow", 256, BF)
        OT = [sb(f"OT{i}", 256) for i in two]
        rs, cn, cT = [sb(f"rs{i}", 32, F32, 64) for i in two], [sb(f"cn{i}", 256, F32, 64) for i in two], [sb(f"cT{i}", 128) for i in two]
        r2, x2, x2b = sb("r2", 512), sb("x2", 512), [sb(f"x2b{i}", 512) for i in two]
        x2h, x2l = [sb(f"x2h{i}", 512, F16) for i in two], [sb(f"x2l{i}", 512, F16) for i in two]
        g, gn, gT = [sb(f"g{i}", 512) for i in range(4)], [sb(f"gn{i}", 512) for i in two], [sb(f"gT{i}", 512) for i in two]
        r3, yo = sb("r3", 512), [sb(f"yo{i}", 512) for i in two]
        stats = {k: (sb("st" + k, 24), sb("mv" + k, 8), sb("ve" + k, 4), sb("rstd" + k, 4)) for k in "1234"}

        V4 = Vblk[:, :].rearrange("p (n c) -> p n c", c=32)
        vz = add("pool", lambda e: e.memset(Vblk[:, :], 0.0), sig="const_pool")
        v1 = add("pool", lambda e: e.memset(V4[0:64, :, 8:9], 1.0), [vz], sig="const_pool")
        v2 = add("pool", lambda e: e.memset(V4[64:128, :, 17:18], 1.0), [v1], sig="const_pool")
        vset = add("pool", lambda e: e.memset(Mrow[64:128, :], 0.0), [v2], sig="const_pool")

        last = {"Qblk": prepared, ("PT", 0): prepared, ("PT", 1): prepared}
        got = {}

        def loads_x(s):
            p = s % 2
            got["xs", s] = add("sp", lambda e: e.dma_start(xs[p][:, :], a["x_nat"][s]), last.get(("xs", p), ()), sig=f"dma_xs{p}", inc=16)
            got["xT", s] = add("sp", lambda e: e.dma_start(xT[p][:, :], a["xT"][s]), last.get(("xT", p), ()), sig=f"dma_xT{p}", inc=16)

        def loads_c(s):
            p = s % 2
            got["cxT", s] = add("sp", lambda e: e.dma_start(cxT[p][:, :], a["cxT"][s]), last.get(("cxT", p), ()), sig=f"dma_cx{p}", inc=16)

        def layernorm(k, src, dst, summed, free, width=128, eps=1e-5):
            st, mv, ve, rstd = stats[k]
            for t in range(4):
                b = add("dve", lambda e, t=t: e.bn_stats(st[:, 6 * t:6 * t + 6], src[:, t * 128:t * 128 + 128]), [summed[t], *last.get(("st", k), ())], sig="ln_st" + k)
            for t in range(4):
                m = add("dve", lambda e, t=t: e.bn_aggr(mv[:, 2 * t:2 * t + 2], st[:, 6 * t:6 * t + 6]), [b, *last.get(("st", k), ())], sig="ln_mv" + k)
            v = add("pool", lambda e: e.tensor_scalar(ve[:, :], mv[:, 1::2], eps, 1.0, ALU.add, ALU.mult), [m], sig="ln_ve" + k)
            r = add("pool", lambda e: e.tensor_tensor(rstd[:, :], ve[:, :], mhalf[:, :], ALU.pow), [v, o2], sig="ln_r" + k)
            done = []
            for t in range(4):
                done.append(add("dve", lambda e, t=t: e.tensor_scalar(
                    dst[:, t * 128:t * 128 + 128], src[:, t * 128:t * 128 + 128], mv[:, 2 * t:2 * t + 1], rstd[:, t:t + 1], ALU.subtract, ALU.mult),
                    [r, m, *free], sig="ln_x" + k))
            last["st", k] = (done[-1],)
            return done

        def stage_a(s):
            p = s % 2
            h = {}
            ch = []

            def kexp(t):
                i, bk, fr = PA.get()
                m = add("pe", lambda e: e.matmul(bk[:, :], xT[p][:, t * 128:t * 128 + 128], Wkf[:, :], start=True, stop=True),
                        [got["xT", s], *prepared, *fr], sig="a_k")
                h["k", t] = add("act", lambda e: e.activation(kp[:, t * 512:t * 512 + 512], bk[:, :], ACT.Exp),
                                [m, *last.get("kp", ())], sig="a_kexp")
                PA.free(i, h["k", t])

            def qexp(g_):
                i, bk, fr = PA.get()
                m = add("pe", lambda e: e.matmul(bk[:, :], Wqf[:, g_ * 128:g_ * 128 + 128], xT[p][:, :], start=True, stop=True),
                        [got["xT", s], *fr], sig="a_q")
                if g_ == 3:
                    last["xT", p] = (m,)
                h["q", g_] = add("act", lambda e: e.activation(qT[p][:, g_ * 512:g_ * 512 + 512], bk[:, :], ACT.Exp, bias=qb[:, g_:g_ + 1]),
                                 [m, *last.get(("qT", p), ())], sig="a_qexp")
                PA.free(i, h["q", g_])

            def ksum():
                i, bk, fr = PA.get()
                for t in range(4):
                    m = add("pe", lambda e, t=t: e.matmul(bk[32 * t:32 * t + 32, :], onesblk[:, :], kp[:, t * 512:t * 512 + 512], start=True, stop=True),
                            [h["k", t], *fr], sig="a_ks")
                d = add("dve", lambda e: e.tensor_tensor(kblkT[:, :], bk[:, :], hmask[:, :], ALU.mult), [m, *last.get("kblkT", ())], sig="a_kbT")
                PA.free(i, d)
                h["kblkT"] = d

            def ksumT():
                i, bk, fr = PA.get()
                for g_ in range(4):
                    m = add("pe", lambda e, g_=g_: e.transpose(bk[:, g_ * 128:g_ * 128 + 128], kblkT[:, g_ * 128:g_ * 128 + 128], ident[:, :]),
                            [h["kblkT"], *fr], sig="a_ksT")
                last["kblkT"] = (m,)
                h["kblk"] = add("act", lambda e: e.activation(kblk[:, :], bk[:, :], ACT.Copy), [m, *last.get("kblk", ())], sig="a_kb")
                PA.free(i, h["kblk"])

            def den():
                i, bk, fr = PA.get()
                for g_ in range(4):
                    m = add("pe", lambda e, g_=g_: e.matmul(bk[:, :], kblk[:, g_ * 128:g_ * 128 + 128], qT[p][:, g_ * 512:g_ * 512 + 512], start=(g_ == 0), stop=(g_ == 3)),
                            [h["kblk"], h["q", g_], *fr], sig="a_den")
                last["kblk"] = (m,)
                d1 = add("dve", lambda e: e.tensor_scalar(Dn[:, :], bk[:, :], 1e-6, None, ALU.add), [m, *last.get("Dn", ())], sig="a_d")
                PA.free(i, d1)
                d2 = add("dve", lambda e: e.reciprocal(Dn[:, :], Dn[:, :]), [d1], sig="a_d")
                h["Dn"] = add("dve", lambda e: e.tensor_tensor(Dn[:, :], Dn[:, :], dmask[:, :], ALU.mult), [d2], sig="a_d")

            def qnorm(g_):
                i, bk, fr = PA.get()
                m = add("pe", lambda e: e.matmul(bk[:, :], hmask[:, g_ * 128:g_ * 128 + 128], Dn[:, :], start=True, stop=True), [h["Dn"], *fr], sig="a_bc")
                sl = slice(g_ * 512, g_ * 512 + 512)
                h["qn", g_] = add("dve", lambda e: e.tensor_tensor(qT[p][:, sl], qT[p][:, sl], bk[:, :], ALU.mult), [m, h["q", g_]], sig="a_qn")
                PA.free(i, h["qn", g_])

            def gmat(b):
                t, r0 = b // 2, 64 * (b % 2)
                i, bk, fr = PA.get()
                m = add("pe", lambda e: e.matmul(bk[:, :], xs[p][r0:r0 + 64, t * 128:t * 128 + 128], kp[r0:r0 + 64, t * 512:t * 512 + 512], start=True, stop=True),
                        [got["xs", s], h["k", t], *fr], sig="a_g")
                if b == 7:
                    last["kp"] = (m,)
                    h["gend"] = m
                n = b % 3
                eng, f = (("act", lambda e: e.activation(GT[n][:, :], bk[:, :], ACT.Copy)) if b % 2 else ("dve", lambda e: e.tensor_copy(GT[n][:, :], bk[:, :])))
                h["G", b] = add(eng, f, [m, *last.get(("GT", n), ())], sig="a_ge_" + eng)
                PA.free(i, h["G", b])

            def cmat(b):
                i, bk, fr = PA.get()
                n, n4 = b % 3, b % 4
                for hh in range(H):
                    g_, j = hh // 4, hh % 4
                    m = add("pe", lambda e, hh=hh, g_=g_, j=j: e.matmul(
                        bk[32 * j:32 * j + 32, g_ * 128:g_ * 128 + 128], GT[n][:, hh * 32:hh * 32 + 32], Mh[:, hh * 128:hh * 128 + 128], start=True, stop=True),
                        [h["G", b], *fr] if hh == 0 else (), sig="a_c" if hh == 15 else None)
                last["GT", n] = (m,)
                eng, f = (("dve", lambda e: e.tensor_copy(Cb[n4][:, :], bk[:, :])) if b % 2 else ("act", lambda e: e.activation(Cb[n4][:, :], bk[:, :], ACT.Copy)))
                h["C", b] = add(eng, f, [m, *last.get(("Cb", n4), ())], sig="a_ce_" + eng)
                PA.free(i, h["C", b])

            def outp(t):
                i, bk, fr = PA.get()
                for bb in range(2):
                    add("pe", lambda e, bb=bb: e.matmul(bk[64 * bb:64 * bb + 64, 0:128], Dn[:, t * 128 + 64 * bb:t * 128 + 64 * bb + 64], nbeta[:, :], start=True, stop=False),
                        [h["Dn"], *fr])
                for g_ in range(4):
                    for bb in range(2):
                        b = 2 * t + bb
                        m = add("pe", lambda e, g_=g_, bb=bb, b=b: e.matmul(
                            bk[64 * bb:64 * bb + 64, 0:128], qT[p][:, g_ * 512 + b * 64:g_ * 512 + b * 64 + 64], Cb[b % 4][:, g_ * 128:g_ * 128 + 128],
                            start=False, stop=(g_ == 3)), [h["C", b], h["qn", g_]], sig="a_o" if (g_, bb) == (3, 1) else None)
                for bb in range(2):
                    last["Cb", (2 * t + bb) % 4] = (m,)
                if t == 3:
                    last["qT", p] = (m,)
                    last["Dn"] = (m,)
                h["r", t] = add("dve", lambda e: e.tensor_tensor(r1[:, t * 128:t * 128 + 128], bk[:, 0:128], xb[:, t * 128:t * 128 + 128], ALU.add),
                                [m, h["xb"], *last.get("r1", ())], sig="a_r")
                PA.free(i, h["r", t])

            def xbias():
                o = xb[:, :].rearrange("p (t d) -> p t d", t=4)
                h["xb"] = add("pool", lambda e: e.tensor_tensor(o, xs[p][:, :].rearrange("p (t d) -> p t d", t=4), biasA[:, :].unsqueeze(1).to_broadcast([128, 4, 128]), ALU.add),
                              [got["xs", s], vset, *prepared, *last.get("xb", ())], sig="a_xb")

            def norm():
                last["xb"] = (h["r", 3],)
                last["xs", p] = (h["gend"], h["xb"])
                x = layernorm("1", r1, x1, [h["r", t] for t in range(4)], last.get("x1", ()))
                last["r1"] = (x[-1],)
                h["x"] = x
                got["x1b", s] = add("pool", lambda e: e.tensor_tensor(x1b[p][:, :].rearrange("p (t d) -> p t d", t=4), x1[:, :].rearrange("p (t d) -> p t d", t=4),
                                                                    bias2[:, :].unsqueeze(1).to_broadcast([128, 4, 128]), ALU.add),
                                    [x[-1], *last.get(("x1b", p), ())], sig="a_x1b")

            def flip():
                i, bk, fr = PA.get()
                for t in range(4):
                    m = add("pe", lambda e, t=t: e.transpose(bk[:, t * 128:t * 128 + 128], x1[:, t * 128:t * 128 + 128], ident[:, :]), [h["x"][t], *fr], sig="a_xT")
                last["x1"] = (m, got["x1b", s])
                got["x1T", s] = add("act", lambda e: e.activation(x1T[p][:, :], bk[:, :], ACT.Copy), [m, *last.get(("x1T", p), ())], sig="a_x1T")
                PA.free(i, got["x1T", s])

            ch.append(xbias)
            for t in range(4):
                ch.append(lambda t=t: kexp(t))
            ch.append(ksum)
            for g_ in range(4):
                ch.append(lambda g_=g_: qexp(g_))
                if g_ == 1:
                    ch.append(ksumT)
            ch.append(lambda: gmat(0))
            ch.append(den)
            ch.append(lambda: cmat(0))
            ch.append(lambda: gmat(1))
            for g_ in range(4):
                ch.append(lambda g_=g_: qnorm(g_))
            for b in range(1, 8):
                ch.append(lambda b=b: cmat(b))
                if b < 7:
                    ch.append(lambda b=b: gmat(b + 1))
                if b % 2:
                    ch.append(lambda b=b: outp(b // 2))
            ch.append(norm)
            ch.append(flip)
            return ch

        def stage_b(s):
            p = s % 2
            h = {}
            ch = []

            Q5 = Qblk[:, :].rearrange("p (g b j n) -> p g b j n", g=4, b=8, j=4)

            def proj(W, src, ready, bias, low, lowb, n, sl, free):
                i, bk, fr = PB.get()
                m = add("pe", lambda e: e.matmul(bk[:, :], W, src, start=True, stop=True), [ready, *fr], sig="b_p")
                hi = add("act", lambda e: e.activation(Qh[n][:, :], bk[:, :], ACT.Identity, bias=lowb, scale=low[:, 0:1]), [m, *last.get(("Qh", n), ())], sig="b_hi")
                r = add("dve", lambda e: e.scalar_tensor_tensor(sl, bk[:, :], bias, Qh[n][:, :], ALU.add, ALU.subtract), [hi, *free], sig="b_sp")
                PB.free(i, r)
                last["Qh", n] = (r,)
                return m, r

            def qproj(g_):
                n = g_ % 2
                m, r = proj(xWq[:, g_ * 128:g_ * 128 + 128], x1T[p][:, :], got["x1T", s], xbq[:, g_:g_ + 1], lowq, xbql[:, g_:g_ + 1], n, Qs[n][:, :], last.get(("Qs", n), ()))
                if g_ == 3:
                    last["x1T", p] = (m,)
                for j in range(4):
                    k = add("dve", lambda e, j=j: e.tensor_scalar(Q5[:, g_, :, j, :], Qs[n][:, :].rearrange("p (b n) -> p b n", b=8), jm[:, j:j + 1], None, ALU.mult), [r, *last.get("Qblk", ())], sig="b_qb")
                h["Q", g_] = k
                last["Qs", n] = (k,)

            def kproj(g_):
                m, h["K", g_] = proj(xWk[:, g_ * 128:g_ * 128 + 128], cxT[p][:, :], got["cxT", s], xbk[:, g_:g_ + 1], lowk, xbkl[:, g_:g_ + 1], g_ % 2,
                                     Ks[:, g_ * 512:g_ * 512 + 512], last.get("Ks", ()))

            def vproj():
                i, bk, fr = PB.get()
                for t in range(4):
                    m = add("pe", lambda e, t=t: e.matmul(bk[:, t * 128:t * 128 + 128], cxT[p][:, t * 128:t * 128 + 128], xWv[:, :], start=True, stop=True),
                            [got["cxT", s], *fr], sig="b_v")
                last["cxT", p] = (m,)
                b3 = bk[:, :].rearrange("p (n c) -> p n c", c=8)
                v = [add("act", lambda e: e.activation(V4[0:64, :, 0:8], b3[0:64], ACT.Copy), [m, vset, *last.get("V", ())], sig="b_ve"),
                     add("act", lambda e: e.activation(V4[64:128, :, 9:17], b3[64:128], ACT.Copy), (), sig="b_ve")]
                h["V"] = v[1]
                PB.free(i, v[1])

            def score(b):
                i, bk, fr = PB.get()
                for g_ in range(4):
                    for jj in range(2):
                        m = add("pe", lambda e, g_=g_, jj=jj: e.matmul(
                            bk[:, (2 * g_ + jj) * 64:(2 * g_ + jj) * 64 + 64], Q5[:, g_, b, 2 * jj:2 * jj + 2, :],
                            Ks[:, g_ * 512 + b * 64:g_ * 512 + b * 64 + 64], start=True, stop=True),
                            [h["Q", g_], h["K", g_], *fr], sig="b_s" if (g_, jj) == (3, 1) else None)
                h["mx", b] = add("dve", lambda e: e.tensor_reduce(mx[:, b * 8:b * 8 + 8], bk[:, :].rearrange("p (n k) -> p n k", k=64), AX.X, ALU.max),
                                 [m, *last.get("mx", ())], sig="b_mx")
                PB.free(i, h["mx", b])

            def rows():
                i, bk, fr = PB.get()
                m = add("pe", lambda e: e.transpose(bk[0:64, 0:128], mx[:, :], ident[:, :]), [h["mx", 7], *fr], sig="b_mT")
                last["mx"] = (m,)
                h["M"] = add("dve", lambda e: e.tensor_tensor(Mrow[0:64, :].rearrange("p (a n) -> p a n", a=2), bk[0:64, 0:128].unsqueeze(1).to_broadcast([64, 2, 128]),
                                                           jmask2[:, :].rearrange("p (a n) -> p a n", a=2), ALU.mult), [m, *last.get("M", ())], sig="b_M")
                PB.free(i, h["M"])

            def prob(t, hf):
                n = t % 2
                i, bk, fr = PB.get()
                for gg in range(2):
                    g_ = 2 * hf + gg
                    for bb in range(2):
                        b = 2 * t + bb
                        o = bk[64 * bb:64 * bb + 64, gg * 256:gg * 256 + 256]
                        add("pe", lambda e, o=o, g_=g_, b=b: e.matmul(o, Ks[:, g_ * 512 + b * 64:g_ * 512 + b * 64 + 64], Q5[:, g_, b, :, :], start=True, stop=False),
                            [h["M"], vset, *fr])
                    for bb in range(2):
                        b = 2 * t + bb
                        o = bk[64 * bb:64 * bb + 64, gg * 256:gg * 256 + 256]
                        c = (b * 4 + g_) * 64
                        m = add("pe", lambda e, o=o, c=c: e.matmul(o, sel[:, c:c + 64], Mrow[:, :], start=False, stop=True), (), sig="b_st")
                if (t, hf) == (3, 1):
                    last["M"] = last["Qblk"] = last["Ks"] = (m,)
                h["P", t, hf] = add("act", lambda e: e.activation(PT[n][:, hf * 512:hf * 512 + 512], bk[:, :], ACT.Exp, scale=SM), [m, *last.get(("PT", n), ())], sig="b_exp")
                PB.free(i, h["P", t, hf])

            def pv(t):
                n = t % 2
                i, bk, fr = PB.get()
                for hh in range(H):
                    g_, j = hh // 4, hh % 4
                    m = add("pe", lambda e, hh=hh, g_=g_, j=j: e.matmul(bk[32 * j:32 * j + 32, g_ * 64:g_ * 64 + 64], V4[:, t * 16 + hh, :], PT[n][:, hh * 64:hh * 64 + 64],
                                                                    start=True, stop=True), [h["P", t, 0], h["P", t, 1], h["V"], *fr] if hh == 0 else (), sig="b_pv" if hh == 15 else None)
                last["PT", n] = (m,)
                if t == 3:
                    last["V"] = (m,)
                h["O", t] = add("dve", lambda e: e.tensor_copy(OT[n][:, :], bk[:, 0:256]), [m, *last.get(("OT", n), ())], sig="b_oe")
                PB.free(i, h["O", t])

            def unflip(t):
                n = t % 2
                i, bk, fr = PB.get()
                for g_ in range(4):
                    m = add("pe", lambda e, g_=g_: e.transpose(bk[0:64, g_ * 128:g_ * 128 + 128], OT[n][:, g_ * 64:g_ * 64 + 64], ident[:, :]), [h["O", t], *fr], sig="b_tr")
                last["OT", n] = (m,)
                b3 = bk[0:64, :].rearrange("p (h c) -> p h c", c=32)
                r3_ = rs[n][:, :].rearrange("p (h c) -> p h c", c=2)
                d = add("dve", lambda e: e.reciprocal(r3_, b3[:, :, 8:18:9]), [m, *last.get(("rs", n), ())], sig="b_rs")
                for bb in range(2):
                    c = add("dve", lambda e, bb=bb: e.tensor_tensor(cn[n][:, bb * 128:bb * 128 + 128].rearrange("p (h c) -> p h c", c=8), b3[:, :, 9 * bb:9 * bb + 8],
                                                              r3_[:, :, bb:bb + 1].to_broadcast([64, 16, 8]), ALU.mult), [d, *last.get(("cn", n), ())], sig="b_cn")
                last["rs", n] = (c,)
                h["c", t] = c
                PB.free(i, c)

            def reflip(t):
                n = t % 2
                i, bk, fr = PB.get()
                for bb in range(2):
                    m = add("pe", lambda e, bb=bb: e.transpose(bk[:, bb * 64:bb * 64 + 64], cn[n][:, bb * 128:bb * 128 + 128], ident[0:64, 0:64]), [h["c", t], *fr], sig="b_tr2")
                last["cn", n] = (m,)
                h["cT", t] = add("act", lambda e: e.activation(cT[n][:, :], bk[:, 0:128], ACT.Copy), [m, *last.get(("cT", n), ())], sig="b_cT")
                PB.free(i, h["cT", t])

            def outp(t):
                n = t % 2
                i, bk, fr = PB.get()
                m = add("pe", lambda e: e.matmul(bk[:, 0:128], cT[n][:, :], xWo[:, :], start=True, stop=True), [h["cT", t], *fr], sig="b_o")
                last["cT", n] = (m,)
                h["r", t] = add("dve", lambda e: e.tensor_tensor(r2[:, t * 128:t * 128 + 128], bk[:, 0:128], x1b[p][:, t * 128:t * 128 + 128], ALU.add),
                                [m, got["x1b", s], *last.get("r2", ())], sig="b_r")
                PB.free(i, h["r", t])
                if t == 3:
                    last["x1b", p] = (h["r", 3],)

            def norm():
                x = layernorm("2", r2, x2, [h["r", t] for t in range(4)], last.get("x2", ()))
                last["r2"] = (x[-1],)
                h["x"] = x
                got["x2b", s] = add("pool", lambda e: e.tensor_tensor(x2b[p][:, :].rearrange("p (t d) -> p t d", t=4), x2[:, :].rearrange("p (t d) -> p t d", t=4),
                                                                    bias3[:, :].unsqueeze(1).to_broadcast([128, 4, 128]), ALU.add),
                                    [x[-1], *last.get(("x2b", p), ())], sig="b_x2b")

            def flip():
                i, bk, fr = PB.get()
                for t in range(4):
                    m = add("pe", lambda e, t=t: e.transpose(bk[:, t * 128:t * 128 + 128], x2[:, t * 128:t * 128 + 128], ident[:, :]), [h["x"][t], *fr], sig="b_xT")
                last["x2"] = (m, got["x2b", s])
                hi = add("act", lambda e: e.activation(x2h[p][:, :], bk[:, :], ACT.Copy), [m, *last.get(("x2T", p), ())], sig="b_x2h")
                got["x2T", s] = add("dve", lambda e: e.tensor_tensor(x2l[p][:, :], bk[:, :], x2h[p][:, :], ALU.subtract), [hi, *last.get(("x2T", p), ())], sig="b_x2l")
                PB.free(i, got["x2T", s])

            for g_ in range(4):
                ch.append(lambda g_=g_: kproj(g_))
                ch.append(lambda g_=g_: qproj(g_))
            ch.append(vproj)
            for b in range(8):
                ch.append(lambda b=b: score(b))
            ch.append(rows)
            ch.append(lambda: prob(0, 0))
            ch.append(lambda: prob(0, 1))
            for t in range(4):
                if t < 3:
                    ch.append(lambda t=t: prob(t + 1, 0))
                    ch.append(lambda t=t: prob(t + 1, 1))
                ch.append(lambda t=t: pv(t))
                if t:
                    ch.append(lambda t=t: reflip(t - 1))
                ch.append(lambda t=t: unflip(t))
                if t:
                    ch.append(lambda t=t: outp(t - 1))
            ch.append(lambda: reflip(3))
            ch.append(lambda: outp(3))
            ch.append(norm)
            ch.append(flip)
            return ch

        def stage_c(s):
            p = s % 2
            h = {}
            ch = []
            st, mv, ve, rstd = stats["4"]

            def up():
                for t in range(4):
                    i, bk, fr = PC.get()
                    sl = slice(t * 128, t * 128 + 128)
                    add("pe", lambda e, bk=bk, sl=sl: e.matmul(bk[:, :], x2h[p][:, sl], tfc[:, :], start=True, stop=False), [got["x2T", s], *fr])
                    m = add("pe", lambda e, bk=bk, sl=sl: e.matmul(bk[:, :], x2l[p][:, sl], tfc[:, :], start=False, stop=True), (), sig="c_up")
                    h["g", t] = add("act", lambda e, bk=bk, t=t: e.activation(g[t][:, :], bk[:, :], ACT.Gelu), [m, *last.get(("g", t), ())], sig="c_g")
                    PC.free(i, h["g", t])
                last["x2T", p] = (m,)

            def stat():
                for t in range(4):
                    b = add("dve", lambda e, t=t: e.bn_stats(st[:, 6 * t:6 * t + 6], g[t][:, :]), [h["g", t], *last.get("st4", ())], sig="c_st")
                for t in range(4):
                    m = add("dve", lambda e, t=t: e.bn_aggr(mv[:, 2 * t:2 * t + 2], st[:, 6 * t:6 * t + 6]), [b], sig="c_mv")
                v = add("pool", lambda e: e.tensor_scalar(ve[:, :], mv[:, 1::2], 1e-5, 1.0, ALU.add, ALU.mult), [m], sig="c_ve")
                h["rstd"] = add("pool", lambda e: e.tensor_tensor(rstd[:, :], ve[:, :], mhalf[:, :], ALU.pow), [v, o2], sig="c_rstd")

            def norm4(t):
                n = t % 2
                h["gn", t] = add("dve", lambda e: e.tensor_scalar(gn[n][:, :], g[t][:, :], mv[:, 2 * t:2 * t + 1], rstd[:, t:t + 1], ALU.subtract, ALU.mult),
                                 [h["rstd"], *last.get(("gn", n), ())], sig="c_gn")
                last["g", t] = (h["gn", t],)
                last["st4"] = (h["gn", t],)
                i, bk, fr = PC.get()
                for c in range(4):
                    m = add("pe", lambda e, c=c: e.transpose(bk[:, c * 128:c * 128 + 128], gn[n][:, c * 128:c * 128 + 128], ident[:, :]), [h["gn", t], *fr], sig="c_tr")
                last["gn", n] = (m,)
                h["gT", t] = add("act", lambda e: e.activation(gT[n][:, :], bk[:, :], ACT.Copy), [m, *last.get(("gT", n), ())], sig="c_gT")
                PC.free(i, h["gT", t])

            def down(t):
                n = t % 2
                i, bk, fr = PC.get()
                for c in range(4):
                    m = add("pe", lambda e, c=c: e.matmul(bk[:, 0:128], gT[n][:, c * 128:c * 128 + 128], Aw[:, c * 128:c * 128 + 128], start=(c == 0), stop=(c == 3)),
                            [h["gT", t], *fr] if c == 0 else (), sig="c_dn" if c == 3 else None)
                last["gT", n] = (m,)
                h["r", t] = add("dve", lambda e: e.tensor_tensor(r3[:, t * 128:t * 128 + 128], bk[:, 0:128], x2b[p][:, t * 128:t * 128 + 128], ALU.add),
                                [m, got["x2b", s], *last.get("r3", ())], sig="c_r")
                PC.free(i, h["r", t])
                if t == 3:
                    last["x2b", p] = (h["r", 3],)

            def norm():
                x = layernorm("3", r3, yo[p], [h["r", t] for t in range(4)], last.get(("yo", p), ()))
                last["r3"] = (x[-1],)
                got["y", s] = add("sp", lambda e: e.dma_start(out[s], yo[p][:, :]), [x[-1]], sig=f"dma_y{p}", inc=16)
                last["yo", p] = (got["y", s],)

            ch.append(up)
            ch.append(stat)
            for t in range(4):
                ch.append(lambda t=t: norm4(t))
                if t:
                    ch.append(lambda t=t: down(t - 1))
            ch.append(lambda: down(3))
            ch.append(norm)
            return ch

        loads_x(0)
        loads_x(1)
        loads_c(0)
        for step in range(NG + 2):
            parts = []
            if 0 <= step - 2 < NG:
                parts.append(stage_c(step - 2))
            if 0 <= step - 1 < NG:
                parts.append(stage_b(step - 1))
            if step < NG:
                parts.append(stage_a(step))
            order = sorted(((k + 0.5) / len(ch), n, k) for n, ch in enumerate(parts) for k in range(len(ch)))
            for _, n, k in order:
                parts[n][k]()
            if step + 1 < NG:
                loads_c(step + 1)
            if step + 2 < NG:
                loads_x(step + 2)
        add("sp", lambda e: e.nop(), [got["y", NG - 2], got["y", NG - 1]])

        block = ctx.enter_context(nc.Block())

        @block.sync
        def _(e):
            q.emit("sp", e)

        @block.gpsimd
        def _(e):
            q.emit("pool", e)

        @block.scalar
        def _(e):
            q.emit("act", e)

        @block.vector
        def _(e):
            q.emit("dve", e)

        @block.tensor
        def _(e):
            q.emit("pe", e)


def constants():
    f = np.float32
    p = np.arange(128)
    c = {}
    c["ident"] = np.eye(128, dtype=f)
    c["hmask"] = (p[:, None] % 16 == np.arange(512)[None, :] // 32).astype(f)
    c["dmask"] = (p[:, None] // 16 == np.arange(512)[None, :] // 64).astype(f)
    c["onesblk"] = (p[:, None] // 64 == np.arange(32)[None, :] // 16).astype(f)
    c["lowq"] = (p % 32 // 8 == 1).astype(f)[:, None].copy()
    c["lowk"] = (p % 32 // 8 == 2).astype(f)[:, None].copy()
    c["jm"] = (p[:, None] // 32 == np.arange(4)[None, :]).astype(f)
    r = np.arange(64)
    sel = -(p[:, None, None] // 2 == np.arange(32)[None, :, None]).astype(f) * np.ones((1, 1, 64), f)
    c["sel"] = sel.reshape(128, 2048)
    c["jmask2"] = (r[:, None] % 2 == np.arange(256)[None, :] // 128).astype(f)
    return c


def kernel(**inputs):
    import concourse.bacc as bacc
    from concourse.bass_utils import run_bass_kernel_spmd as run

    w = {k: np.asarray(v) for k, v in inputs.items()}
    f = np.float32
    A = {}
    A["x_nat"] = w["x"].reshape(NG, 4, 128, D).transpose(0, 2, 1, 3).reshape(NG, 128, 512)
    A["xT"] = w["x"].reshape(NG, 512, D).transpose(0, 2, 1)
    A["cxT"] = w["ctx_1024"].reshape(NG, 512, D).transpose(0, 2, 1)

    def pairs(W):
        return W.reshape(8, 128, -1).transpose(1, 0, 2).reshape(128, -1)

    for k in "qkv":
        A[f"W{k}T"] = pairs(w[f"L0_attn_W{k}"].T)
    for k in "qk":
        m = np.zeros((128, 64), f)
        m[0:64, 0:32] = w[f"L0_attn_w{k}_feat"]
        m[64:128, 32:64] = w[f"L0_attn_w{k}_feat"]
        A[f"feat{k}"] = m
        A[f"b{k}T"] = w[f"L0_attn_b{k}"].reshape(8, 128).T
    A["Wpj"] = pairs(w["L0_attn_Wproj"])
    bv = w["L0_attn_bv"].reshape(8, 2, 64)
    blk = np.zeros((2, 64, 8, 8, 16), f)
    for c in range(8):
        for hp in range(2):
            blk[hp, :, c, :, 2 * c + hp] = bv[c, hp][:, None]
    A["bvblk"] = blk.reshape(128, 1024)
    A["bvrep"] = np.repeat(w["L0_attn_bv"].reshape(8, 128).T[:, :, None], 128, axis=2).reshape(128, 1024)
    A["bproj"] = w["L0_attn_bproj"].reshape(1, 128)
    A["bo"] = w["L0_xattn_bo"].reshape(1, 128)
    for k, low in (("q", 1), ("k", 2)):
        W = w[f"L0_xattn_W{k}"].T.reshape(128, 4, 4, 8)
        m = np.zeros((128, 4, 4, 4, 8), f)
        b = np.zeros((4, 4, 8, 4), f)
        bl = np.zeros((4, 4, 8, 4), f)
        bb = w[f"L0_xattn_b{k}"].reshape(4, 4, 8).transpose(1, 2, 0)
        for rep in range(3):
            m[:, :, :, rep, :] = W
            b[:, rep] = bb
        bl[:, low] = bb
        A[f"xW{k}"] = m.reshape(128, 512)
        A[f"xb{k}"] = b.reshape(128, 4)
        A[f"xb{k}l"] = bl.reshape(128, 4)
    A["xWv"] = w["L0_xattn_Wv"].T
    A["xWo"] = w["L0_xattn_Wo"].T
    A["xbvrep"] = np.repeat(w["L0_xattn_bv"][:, None], 128, axis=1)
    A["Wfc"] = w["L0_ffn_W_fc"].T
    A["Wpr"] = w["L0_ffn_W_proj"].T.reshape(4, 128, 128).transpose(1, 0, 2).reshape(128, 512)
    A["lnw"] = w["L0_ffn_ln_w"].reshape(4, 128).T
    A["lnbrep"] = np.repeat(w["L0_ffn_ln_b"].reshape(4, 128).T[:, :, None], 128, axis=2).reshape(128, 512)
    A.update(constants())

    nc = bacc.Bacc("TRN2", target_bir_lowering=False, num_devices=1)
    arrays, aps = {}, {}
    for name, v in A.items():
        v = np.ascontiguousarray(v)
        arrays["in_" + name] = v
        aps[name] = nc.dram_tensor("in_" + name, v.shape, mybir.dt.from_np(v.dtype), kind="ExternalInput").ap()
    o = nc.dram_tensor("out_y", (NG, 128, 512), mybir.dt.float32, kind="ExternalOutput").ap()
    decoder_kernel(nc, aps, o)
    r = run(nc, [arrays], core_ids=[0])
    y = np.asarray(r.results[0]["out_y"])
    return y.reshape(NG, 128, 4, D).transpose(0, 2, 1, 3).reshape(NB, T, D)
```

```python
import numpy as np
import concourse.bass as bass
from concourse import mybir
from contextlib import ExitStack

NB = 128
T = 64
D = 128
NG = 16
H = 16


class Queues:

    def __init__(self, nc, ctx):
        self.nc, self.ctx = nc, ctx
        self.sems, self.count = {}, {}
        self.lists = {e: [] for e in ("pe", "act", "dve", "pool", "sp")}

    def add(self, eng, fn, waits=(), sig=None, inc=1):
        done = None
        if sig is not None:
            if sig not in self.sems:
                self.sems[sig] = self.ctx.enter_context(self.nc.semaphore("s_" + sig))
                self.count[sig] = 0
            self.count[sig] += inc
            done = (sig, self.count[sig])
        self.lists[eng].append((fn, tuple(w for w in waits if w is not None), sig, inc))
        return done

    def emit(self, eng, e):
        seen = {}
        for fn, waits, sig, inc in self.lists[eng]:
            need = {}
            for name, value in waits:
                need[name] = max(need.get(name, 0), value)
            for name, value in need.items():
                if seen.get(name, 0) < value:
                    e.wait_ge(self.sems[name], value)
                    seen[name] = value
            ins = fn(e)
            if sig is not None:
                ins.then_inc(self.sems[sig], inc)


class Banks:

    def __init__(self, banks):
        self.banks, self.freed, self.n = banks, [()] * len(banks), 0

    def get(self):
        i = self.n % len(self.banks)
        self.n += 1
        return i, self.banks[i], self.freed[i]

    def free(self, i, *reads):
        self.freed[i] = reads


def decoder_kernel(nc, a, out):
    F32, F16, BF = mybir.dt.float32, mybir.dt.float16, mybir.dt.bfloat16
    ALU, ACT, AX = mybir.AluOpType, mybir.ActivationFunctionType, mybir.AxisListType
    SM = 8.0 ** -0.5

    with ExitStack() as ctx:
        q = Queues(nc, ctx)
        add = q.add

        def sb(name, cols, dt=F32, parts=128):
            return ctx.enter_context(nc.sbuf_tensor(name, [parts, cols], dt))

        banks = [ctx.enter_context(nc.psum_tensor(f"bank{i}", [128, 512], F32)) for i in range(8)]
        PS = Banks(banks)

        held = {}

        def load(name, dt=F32, t=None):
            shape = a[name].shape
            if t is None:
                t = sb("w_" + name, shape[1], dt, shape[0])
            add("sp", lambda e, t=t, n=name: e.dma_start(t[:, :], a[n]), sig="weights", inc=16)
            held[name] = t
            return t

        two = range(2)
        Qblk, PT, kp = [sb(f"Qblk{i}", 8192, F16) for i in two], [sb(f"PT{i}", 1024) for i in two], sb("kp", 2048)
        late = [Qblk[n][:, 2048 * i:2048 * i + 2048].bitcast(F32) for n in two for i in range(4)]
        WqT, WkT, WvT, Wpj = [load(n, t=late[i]) for i, n in enumerate(("WqT", "WkT", "WvT", "Wpj"))]
        Wfc, Wpr = load("Wfc", t=late[4][:, 0:512]), load("Wpr", t=late[4][:, 512:1024])
        lnb = load("lnbrep", t=late[5][:, 0:512])
        tmp, tpr, brow = late[5][:, 512:1024], late[6][:, 0:512], [late[6][0:1, 512:1024], late[7][0:1, 0:512], late[7][0:1, 512:1024]]
        bvblk, bvrep = load("bvblk", t=PT[0]), load("bvrep", t=PT[1])
        fq, fk = load("featq"), load("featk")
        bqT, bkT = load("bqT"), load("bkT")
        bpj, bo = load("bproj"), load("bo")
        xWq, xWk, xbq, xbk = load("xWq"), load("xWk"), load("xbq"), load("xbk")
        xWv, xWo, xbv = load("xWv"), load("xWo"), load("xbvrep")
        lnw, ident, ones2, jm = load("lnw"), load("ident"), load("ones2"), load("jm")
        place = {k: load("place_" + k, F16) for k in ("qh", "ql", "kh", "kl")}
        tmask, kone = load("tmask"), load("kone")
        n_w = len(held)
        weights = ("weights", 16 * n_w)

        ones = sb("ones", 128)
        mhalf = sb("mhalf", 4)
        o1 = add("dve", lambda e: e.memset(ones[:, :], 1.0), sig="const")
        o2 = add("dve", lambda e: e.memset(mhalf[:, :], -0.5), sig="const")

        Mh = sb("Mh", 2048)
        Wqf, Wkf = [(sb(f"W{k}fh", 512, F16), sb(f"W{k}fl", 512, F16)) for k in "qk"]
        onesb, qbias = sb("onesb", 128, BF), sb("qbias", 512, BF)
        nbeta, biasA, bias2, bias3 = sb("nbeta", 512), sb("biasA", 128), sb("bias2", 128), sb("bias3", 128)
        tfc, tpj, identh = sb("tfc", 512, F16), sb("tpj", 512, F16), sb("identh", 128, F16)
        o3 = add("dve", lambda e: e.memset(onesb[:, :], 1.0), sig="const")
        o4 = add("dve", lambda e: e.memset(qbias[:, :], 0.0), sig="const")

        def prep():
            def pe(fns, waits, sig="w_pe"):
                for f in fns[:-1]:
                    add("pe", f, waits)
                    waits = ()
                return add("pe", fns[-1], waits, sig=sig)

            ready = []
            for W, f, dst in ((WqT, fq, Wqf), (WkT, fk, Wkf)):
                i, bk, fr = PS.get()
                m = pe([lambda e, W=W, f=f, bk=bk, c=c: e.matmul(bk[:, c * 64:c * 64 + 64], W[:, c * 128:c * 128 + 128], f[:, :], start=True, stop=True)
                        for c in range(8)], [weights, *fr])
                r = add("act", lambda e, bk=bk, dst=dst: e.activation(dst[0][:, :], bk[:, :], ACT.Copy), [m], sig="w_act")
                r = add("dve", lambda e, bk=bk, dst=dst: e.tensor_tensor(dst[1][:, :], bk[:, :], dst[0][:, :], ALU.subtract), [r], sig="w_dve")
                PS.free(i, r)
                ready.append(r)
            i, bk, fr = PS.get()
            fns = []
            for c in range(8):
                o = bk[0:1, c * 64:c * 64 + 64]
                fns.append(lambda e, o=o, c=c: e.matmul(o, bqT[:, c:c + 1], fq[:, :], start=True, stop=False))
                fns.append(lambda e, o=o, c=c: e.matmul(o, bkT[:, c:c + 1], fk[:, :], start=False, stop=True))
            m = pe(fns, fr)
            rest = [bk[0:1, :], brow[0], brow[1]]
            r = o4
            for n in range(3):
                o = qbias[32 * n:32 * n + 1, :]
                r = add("dve", lambda e, n=n, o=o: e.tensor_copy(o, rest[n]), [m, r], sig="w_dve")
                if n < 2:
                    r = add("dve", lambda e, n=n, o=o: e.tensor_copy(brow[2], o), [r], sig="w_dve")
                    r = add("dve", lambda e, n=n, o=o: e.tensor_tensor(rest[n + 1], rest[n], brow[2], ALU.subtract), [r], sig="w_dve")
            PS.free(i, r)
            ready.append(r)
            for c in range(4):
                i, bk, fr = PS.get()
                fns = []
                hp, r0 = c % 2, 64 * (c % 2)
                for k in range(4):
                    w = slice((4 * (c // 2) + k) * 128, (4 * (c // 2) + k) * 128 + 128)
                    fns.append(lambda e, bk=bk, k=k, w=w, r0=r0: e.matmul(
                        bk[:, k * 128:k * 128 + 128], WvT[r0:r0 + 64, w], Wpj[r0:r0 + 64, w], start=True, stop=True))
                m = pe(fns, fr)
                o = Mh[:, :].rearrange("p (c k a n) -> p c k a n", c=2, k=4, a=2)[:, c // 2, :, hp, :]
                r = add("act", lambda e, bk=bk, o=o: e.activation(o, bk[:, :].rearrange("p (k n) -> p k n", k=4), ACT.Copy), [m], sig="w_act")
                PS.free(i, r)
                ready.append(r)

            def acc(lhs, rhs, row, n):
                fns = [lambda e, c=c, bk=bk: e.matmul(bk[:, 0:128], lhs[:, c * 128:c * 128 + 128], rhs[:, c * 128:c * 128 + 128],
                                                      start=(c == 0), stop=(c == n - 1 and row is None)) for c in range(n)]
                if row is not None:
                    fns.append(lambda e, bk=bk: e.matmul(bk[:, 0:128], ones[0:1, 0:128], row[0:1, :], start=False, stop=True))
                return fns

            for lhs, rhs, row, n, dst, scale in ((bvrep, Wpj, bpj, 8, biasA, 1.0),
                                                 (xbv, xWo, bo, 1, bias2, 1.0)):
                i, bk, fr = PS.get()
                m = pe(acc(lhs, rhs, row, n), [o1, *fr])
                r = add("act", lambda e, bk=bk, dst=dst, scale=scale: e.activation(dst[:, :], bk[:, 0:128], ACT.Copy, scale=scale), [m], sig="w_act")
                PS.free(i, r)
                ready.append(r)
            i, bk, fr = PS.get()
            m = pe(acc(bvblk, Wpj, None, 8), fr)
            for t in range(4):
                r = add("act", lambda e, bk=bk, t=t: e.activation(nbeta[:, t * 128:t * 128 + 128], bk[:, 0:128], ACT.Copy, scale=tmask[:, t:t + 1]), [m], sig="w_act")
            PS.free(i, r)
            ready.append(r)
            colsum, hg = sb("colsum", 2), sb("hg", 4)
            for n, W in enumerate((Wfc, Wpr)):
                c = add("dve", lambda e, n=n, W=W: e.tensor_reduce(colsum[:, n:n + 1], W[:, :], AX.X, ALU.add, apply_absolute_value=True),
                        [weights], sig="w_dve")
            i, bk, fr = PS.get()
            m = pe([lambda e, bk=bk: e.matmul(bk[:, 0:2], ones[:, :], colsum[:, :], start=True, stop=True)], [c, *fr])
            h1 = add("dve", lambda e, bk=bk: e.tensor_scalar(hg[:, 0:2], bk[:, 0:2], 1.0 / 65536, 1e-6, ALU.mult, ALU.add), [m], sig="w_dve")
            PS.free(i, h1)
            h2 = add("dve", lambda e: e.tensor_scalar(hg[:, 2:4], hg[:, 0:2], -0.5, None, ALU.mult), [h1], sig="w_dve")
            h3 = add("dve", lambda e: e.tensor_scalar(hg[:, 0:2], hg[:, 0:2], 0.5, None, ALU.mult), [h2], sig="w_dve")
            for n, (W, dst) in enumerate(((Wfc, tfc), (Wpr, tpr))):
                t1 = add("dve", lambda e, n=n, W=W: e.tensor_scalar(tmp[:, :], W[:, :], hg[:, 2 + n:3 + n], None, ALU.is_lt), [h3], sig="w_dve")
                h3 = add("dve", lambda e, n=n, W=W, dst=dst: e.scalar_tensor_tensor(dst[:, :], W[:, :], hg[:, n:n + 1], tmp[:, :], ALU.is_gt, ALU.subtract),
                         [t1], sig="w_dve")
            ready.append(add("dve", lambda e: e.tensor_copy(tpj[:, :], tpr[:, :]), [h3], sig="w_dve"))
            ready.append(add("dve", lambda e: e.tensor_copy(identh[:, :], ident[:, :]), [h3], sig="w_dve"))
            i, bk, fr = PS.get()
            m = pe(acc(lnb, tpr, None, 4), [h3, *fr])
            r = add("act", lambda e, bk=bk: e.activation(bias3[:, :], bk[:, 0:128], ACT.Copy), [m], sig="w_act")
            PS.free(i, r)
            ready.append(r)
            return ready

        prepared = [o3, *prep()]

        xs, xT, cxT = [sb(f"xs{i}", 512) for i in two], [sb(f"xT{i}", 512) for i in two], [sb(f"cxT{i}", 512) for i in two]
        xh, xl = [sb(f"xh{i}", 512, F16) for i in two], [sb(f"xl{i}", 512, F16) for i in two]
        qn, prod, qT = [sb(f"qn{i}", 512) for i in two], sb("prod", 512), sb("qT", 2048)
        dsum, Dv, DT, xb = sb("dsum", 64), sb("Dv", 128), sb("DT", 128), sb("xb", 512)
        GT, Cb = [sb(f"GT{i}", 512) for i in range(3)], [sb(f"Cb{i}", 512) for i in range(4)]
        x1, x1b, x1T = [sb(f"x1{i}", 512) for i in two], [sb(f"x1b{i}", 512) for i in range(3)], sb("x1T", 512)
        Qh, Ql = [sb(f"Qh{i}", 512, F16) for i in two], [sb(f"Ql{i}", 512, F16) for i in two]
        Qs, Ks = [sb(f"Qs{i}", 512, F16) for i in two], [sb(f"Ks{i}", 2048, F16) for i in two]
        Vblk = [sb(f"Vblk{i}", 2048) for i in two]
        mx, Mrow = [sb(f"mx{i}", 64) for i in two], [sb(f"Mrow{i}", 128, F16, 64) for i in two]
        OT = [sb(f"OT{i}", 256) for i in two]
        rs, cn, cT = [sb(f"rs{i}", 32, F32, 64) for i in two], [sb(f"cn{i}", 256, F32, 64) for i in two], [sb(f"cT{i}", 128) for i in two]
        x2, x2b = [sb(f"x2{i}", 512) for i in two], [sb(f"x2b{i}", 512) for i in two]
        x2h, x2l = sb("x2h", 512, F16), sb("x2l", 512, F16)
        g, gT = [sb(f"g{i}", 512) for i in range(4)], [sb(f"gT{i}", 1024, F16) for i in two]
        gh = [sb(f"gh{i}", 1024, F16) for i in two]
        yo = [sb(f"yo{i}", 512) for i in two]
        stats = {k: (sb("st" + k, 24), sb("mv" + k, 8), sb("ve" + k, 4), sb("rstd" + k, 4)) for k in "1234"}

        V4 = [v[:, :].rearrange("p (n c) -> p n c", c=32) for v in Vblk]
        vset = None
        for n in two:
            vset = add("pool", lambda e, n=n: e.memset(Vblk[n][:, :], 0.0), [vset], sig="const_pool")
            vset = add("pool", lambda e, n=n: e.memset(V4[n][0:64, :, 8:9], 1.0), [vset], sig="const_pool")
            vset = add("pool", lambda e, n=n: e.memset(V4[n][64:128, :, 17:18], 1.0), [vset], sig="const_pool")
        vset = add("pool", lambda e: e.memset(Dv[:, :], 0.0), [vset], sig="const_pool")

        last = {(k, n): prepared for k in ("Qblk", "PT") for n in two}
        got = {}

        def loads_x(s):
            p = s % 2
            got["xs", s] = add("sp", lambda e: e.dma_start(xs[p][:, :], a["x_nat"][s]), last.get(("xs", p), ()), sig=f"dma_xs{p}", inc=16)
            got["xT", s] = add("sp", lambda e: e.dma_start(xT[p][:, :], a["xT"][s]), last.get(("xT", p), ()), sig=f"dma_xT{p}", inc=16)

        def split_x(s):
            p = s % 2
            hi = add("pool", lambda e: e.tensor_copy(xh[p][:, :], xT[p][:, :]), [got["xT", s], vset, *last.get(("xhl", p), ())], sig="a_xh")
            got["xhl", s] = add("pool", lambda e: e.tensor_tensor(xl[p][:, :], xT[p][:, :], xh[p][:, :], ALU.subtract), [hi], sig="a_xl")
            last["xT", p] = (got["xhl", s],)

        def loads_c(s):
            p = s % 2
            got["cxT", s] = add("sp", lambda e: e.dma_start(cxT[p][:, :], a["cxT"][s]), last.get(("cxT", p), ()), sig=f"dma_cx{p}", inc=16)

        def layernorm(k, x, summed, eps=1e-5):
            st, mv, ve, rstd = stats[k]
            for t in range(4):
                b = add("dve", lambda e, t=t: e.bn_stats(st[:, 6 * t:6 * t + 6], x[:, t * 128:t * 128 + 128]), [summed[t], *last.get(("st", k), ())], sig="ln_st" + k)
            for t in range(4):
                m = add("dve", lambda e, t=t: e.bn_aggr(mv[:, 2 * t:2 * t + 2], st[:, 6 * t:6 * t + 6]), [b, *last.get(("st", k), ())], sig="ln_mv" + k)
            v = add("pool", lambda e: e.tensor_scalar(ve[:, :], mv[:, 1::2], eps, 1.0, ALU.add, ALU.mult), [m], sig="ln_ve" + k)
            r = add("pool", lambda e: e.tensor_tensor(rstd[:, :], ve[:, :], mhalf[:, :], ALU.pow), [v, o2], sig="ln_r" + k)
            done = []
            for t in range(4):
                done.append(add("dve", lambda e, t=t: e.tensor_scalar(
                    x[:, t * 128:t * 128 + 128], x[:, t * 128:t * 128 + 128], mv[:, 2 * t:2 * t + 1], rstd[:, t:t + 1], ALU.subtract, ALU.mult),
                    [r, m], sig="ln_x" + k))
            last["st", k] = (done[-1],)
            return done

        def stage_a(s):
            p = s % 2
            h = {}

            def logits(bk, t, W, stop, waits, sig):
                sl = slice(t * 128, t * 128 + 128)
                add("pe", lambda e: e.matmul(bk[:, :], xh[p][:, sl], W[0][:, :], start=True, stop=False), waits)
                add("pe", lambda e: e.matmul(bk[:, :], xh[p][:, sl], W[1][:, :], start=False, stop=False))
                return add("pe", lambda e: e.matmul(bk[:, :], xl[p][:, sl], W[0][:, :], start=False, stop=stop), (), sig=sig)

            def kexp(t):
                i, bk, fr = PS.get()
                m = logits(bk, t, Wkf, True, [got["xhl", s], *prepared, *fr], "a_k")
                h["k", t] = add("act", lambda e: e.activation(kp[:, t * 512:t * 512 + 512], bk[:, :], ACT.Exp),
                                [m, *last.get("kp", ())], sig="a_kexp")
                PS.free(i, h["k", t])

            def qexp(t):
                n = t % 2
                i, bk, fr = PS.get()
                logits(bk, t, Wqf, False, [got["xhl", s], *fr], None)
                m = add("pe", lambda e: e.matmul(bk[:, :], onesb[:, :], qbias[:, :], start=False, stop=True), (), sig="a_q")
                if t == 3:
                    last["xhl", p] = (m,)
                h["q", t] = add("act", lambda e: e.activation(qn[n][:, :], bk[:, :], ACT.Exp), [m, *last.get(("qn", n), ())], sig="a_qexp")
                PS.free(i, h["q", t])

            def ksum(t):
                n = t % 2
                i, bk, fr = PS.get()
                m = add("pe", lambda e: e.matmul(bk[:, :], ones2[:, :], kp[:, t * 512:t * 512 + 512], start=True, stop=True), [h["k", t], *fr], sig="a_ks")
                d = add("dve", lambda e: e.tensor_tensor(prod[:, :], qn[n][:, :], bk[:, :], ALU.mult), [m, h["q", t], *last.get("prod", ())], sig="a_pr")
                PS.free(i, d)
                d = add("dve", lambda e: e.tensor_reduce(dsum[:, t * 16:t * 16 + 16], prod[:, :].rearrange("p (h f) -> p h f", f=32), AX.X, ALU.add), [d], sig="a_ds")
                last["prod"] = (d,)
                d = add("dve", lambda e: e.tensor_scalar(dsum[:, t * 16:t * 16 + 16], dsum[:, t * 16:t * 16 + 16], 1e-6, None, ALU.add), [d], sig="a_ds")
                h["D", t] = add("dve", lambda e: e.reciprocal(Dv[:, t * 16:t * 16 + 16], dsum[:, t * 16:t * 16 + 16]), [d, vset, *last.get("Dv", ())], sig="a_dv")
                v = qn[n][:, :].rearrange("p (h f) -> p h f", f=32)
                h["qn", t] = add("pool", lambda e: e.tensor_tensor(v, v, Dv[:, t * 16:t * 16 + 16].unsqueeze(2).to_broadcast([128, 16, 32]), ALU.mult), [h["D", t], vset], sig="a_qn")

            def qturn(t):
                n = t % 2
                i, bk, fr = PS.get()
                for g_ in range(4):
                    m = add("pe", lambda e, g_=g_: e.transpose(bk[:, g_ * 128:g_ * 128 + 128], qn[n][:, g_ * 128:g_ * 128 + 128], ident[:, :]),
                            [h["qn", t], *fr], sig="a_qT")
                last["qn", n] = (m,)
                o = qT[:, :].rearrange("p (g n) -> p g n", g=4)[:, :, t * 128:t * 128 + 128]
                h["qT", t] = add("act", lambda e: e.activation(o, bk[:, :].rearrange("p (g n) -> p g n", g=4), ACT.Copy), [m, *last.get("qT", ())], sig="a_qTe")
                PS.free(i, h["qT", t])

            def dturn():
                i, bk, fr = PS.get()
                m = add("pe", lambda e: e.transpose(bk[:, 0:128], Dv[:, :], ident[:, :]), [h["D", 3], *fr], sig="a_DT")
                last["Dv"] = (m, h["qn", 3])
                h["DT"] = add("act", lambda e: e.activation(DT[:, :], bk[:, 0:128], ACT.Copy), [m, *last.get("DT", ())], sig="a_DTe")
                PS.free(i, h["DT"])

            def gmat(b):
                t, r0 = b // 2, 64 * (b % 2)
                i, bk, fr = PS.get()
                m = add("pe", lambda e: e.matmul(bk[:, :], xs[p][r0:r0 + 64, t * 128:t * 128 + 128], kp[r0:r0 + 64, t * 512:t * 512 + 512], start=True, stop=True),
                        [got["xs", s], h["k", t], *fr], sig="a_g")
                if b == 7:
                    last["kp"] = (m,)
                    h["gend"] = m
                n = b % 3
                eng, f = (("act", lambda e: e.activation(GT[n][:, :], bk[:, :], ACT.Copy)) if b % 2 else ("dve", lambda e: e.tensor_copy(GT[n][:, :], bk[:, :])))
                h["G", b] = add(eng, f, [m, *last.get(("GT", n), ())], sig="a_ge_" + eng)
                PS.free(i, h["G", b])

            def cmat(b):
                i, bk, fr = PS.get()
                n, n4 = b % 3, b % 4
                for hh in range(H):
                    g_, j = hh // 4, hh % 4
                    m = add("pe", lambda e, hh=hh, g_=g_, j=j: e.matmul(
                        bk[32 * j:32 * j + 32, g_ * 128:g_ * 128 + 128], GT[n][:, hh * 32:hh * 32 + 32], Mh[:, hh * 128:hh * 128 + 128], start=True, stop=True),
                        [h["G", b], *fr] if hh == 0 else (), sig="a_c" if hh == 15 else None)
                last["GT", n] = (m,)
                eng, f = (("dve", lambda e: e.tensor_copy(Cb[n4][:, :], bk[:, :])) if b % 2 else ("act", lambda e: e.activation(Cb[n4][:, :], bk[:, :], ACT.Copy)))
                h["C", b] = add(eng, f, [m, *last.get(("Cb", n4), ())], sig="a_ce_" + eng)
                PS.free(i, h["C", b])

            def outp(t):
                i, bk, fr = PS.get()
                for bb in range(2):
                    add("pe", lambda e, bb=bb: e.matmul(bk[64 * bb:64 * bb + 64, 0:128], DT[:, 64 * bb:64 * bb + 64], nbeta[:, t * 128:t * 128 + 128], start=True, stop=False),
                        [h["DT"], *fr])
                for g_ in range(4):
                    for bb in range(2):
                        b = 2 * t + bb
                        m = add("pe", lambda e, g_=g_, bb=bb, b=b: e.matmul(
                            bk[64 * bb:64 * bb + 64, 0:128], qT[:, g_ * 512 + b * 64:g_ * 512 + b * 64 + 64], Cb[b % 4][:, g_ * 128:g_ * 128 + 128],
                            start=False, stop=(g_ == 3)), [h["C", b], h["qT", t]], sig="a_o" if (g_, bb) == (3, 1) else None)
                for bb in range(2):
                    last["Cb", (2 * t + bb) % 4] = (m,)
                if t == 3:
                    last["qT"] = last["DT"] = (m,)
                h["r", t] = add("dve", lambda e: e.tensor_tensor(x1[p][:, t * 128:t * 128 + 128], bk[:, 0:128], xb[:, t * 128:t * 128 + 128], ALU.add),
                                [m, h["xb"], *last.get(("x1", p), ())], sig="a_r")
                PS.free(i, h["r", t])

            def xbias():
                o = xb[:, :].rearrange("p (t d) -> p t d", t=4)
                h["xb"] = add("pool", lambda e: e.tensor_tensor(o, xs[p][:, :].rearrange("p (t d) -> p t d", t=4), biasA[:, :].unsqueeze(1).to_broadcast([128, 4, 128]), ALU.add),
                              [got["xs", s], vset, *prepared, *last.get("xb", ())], sig="a_xb")

            def norm():
                last["xb"] = (h["r", 3],)
                last["xs", p] = (h["gend"], h["xb"])
                x = layernorm("1", x1[p], [h["r", t] for t in range(4)])
                got["x1", s] = x
                n = s % 3
                got["x1b", s] = add("pool", lambda e: e.tensor_tensor(x1b[n][:, :].rearrange("p (t d) -> p t d", t=4), x1[p][:, :].rearrange("p (t d) -> p t d", t=4),
                                                                    bias2[:, :].unsqueeze(1).to_broadcast([128, 4, 128]), ALU.add),
                                    [x[-1], *last.get(("x1b", n), ())], sig="a_x1b")

            order = [(0.1, xbias)]
            for t in range(4):
                order.append((0.7, lambda t=t: kexp(t)))
                if t < 2:
                    order.append((0.9, lambda t=t: qexp(t)))
            order += [(0.9, lambda: ksum(0)), (0.9, lambda: gmat(0)), (0.9, lambda: ksum(1)), (0.9, lambda: gmat(1)), (1.1, lambda: cmat(0)),
                      (0.5, lambda: qturn(0)), (0.9, lambda: qexp(2)), (0.9, lambda: gmat(2)), (1.1, lambda: cmat(1)), (0.5, lambda: qturn(1)),
                      (0.9, lambda: ksum(2)), (0.9, lambda: qexp(3)), (0.9, lambda: gmat(3)), (1.1, lambda: cmat(2)), (0.9, lambda: ksum(3)),
                      (0.9, lambda: gmat(4)), (0.5, lambda: qturn(2)), (1.1, lambda: cmat(3)), (0.9, lambda: gmat(5)), (0.1, dturn),
                      (0.5, lambda: qturn(3)), (1.2, lambda: outp(0)), (1.1, lambda: cmat(4)), (0.9, lambda: gmat(6)), (1.1, lambda: cmat(5)),
                      (1.2, lambda: outp(1)), (0.9, lambda: gmat(7)), (1.1, lambda: cmat(6)), (1.2, lambda: outp(2)), (1.1, lambda: cmat(7)), (1.50, None),
                      (1.2, lambda: outp(3)), (0.5, norm)]
            return order

        hb = {}
        Q5 = [t[:, :].rearrange("p (g b j n) -> p g b j n", g=4, b=8, j=4) for t in Qblk]

        def stage_b1(s):
            p = s % 2
            h = hb.setdefault(s, {})

            def flip():
                i, bk, fr = PS.get()
                for t in range(4):
                    m = add("pe", lambda e, t=t: e.transpose(bk[:, t * 128:t * 128 + 128], x1[p][:, t * 128:t * 128 + 128], ident[:, :]), [got["x1", s][t], *fr], sig="a_xT")
                last["x1", p] = (m, got["x1b", s])
                h["x1T"] = add("act", lambda e: e.activation(x1T[:, :], bk[:, :], ACT.Copy), [m, *last.get("x1T", ())], sig="a_x1T")
                PS.free(i, h["x1T"])

            def proj(k, W, src, ready, bias):
                n = "qk".index(k)
                i, bk, fr = PS.get()
                m = add("pe", lambda e: e.matmul(bk[:, :], W[:, :], src[:, :], start=True, stop=True), [ready, *fr], sig="b_p")
                free = last.get(("Qh", n), ())
                hi = add("act", lambda e: e.activation(Qh[n][:, :], bk[:, :], ACT.Identity, bias=bias[:, 0:1]), [m, *free], sig="b_hi")
                h["hi" + k] = hi
                h["lo" + k] = add("dve", lambda e: e.scalar_tensor_tensor(Ql[n][:, :], bk[:, :], bias[:, 0:1], Qh[n][:, :], ALU.add, ALU.subtract), [hi, *free], sig="b_lo")
                PS.free(i, h["lo" + k])
                return m

            def spread(k, g_, out, free):
                n = "qk".index(k)
                i, bk, fr = PS.get()
                sl = slice(g_ * 128, g_ * 128 + 128)
                add("pe", lambda e: e.matmul(bk[:, :], place[k + "h"][:, sl], Qh[n][:, :], start=True, stop=False), [h["hi" + k], *fr])
                m = add("pe", lambda e: e.matmul(bk[:, :], place[k + "l"][:, sl], Ql[n][:, :], start=False, stop=True), [h["lo" + k]], sig="b_pl")
                if g_ == 3:
                    last["Qh", n] = (m,)
                f = (lambda e: e.activation(out, bk[:, :], ACT.Copy)) if k == "q" else (lambda e: e.activation(out, bk[:, :], ACT.Identity, bias=kone[:, 0:1]))
                r = add("act", f, [m, *free], sig="b_ple")
                PS.free(i, r)
                return r

            def kproj():
                proj("k", xWk, cxT[p], got["cxT", s], xbk)

            def qproj():
                last["x1T"] = (proj("q", xWq, x1T, h["x1T"], xbq),)

            def kspread(g_):
                h["K", g_] = spread("k", g_, Ks[p][:, g_ * 512:g_ * 512 + 512], last.get(("Ks", p), ()))

            def qspread(g_):
                n = g_ % 2
                r = spread("q", g_, Qs[n][:, :], last.get(("Qs", n), ()))
                for j in range(4):
                    k = add("dve", lambda e, j=j: e.tensor_scalar(Q5[p][:, g_, :, j, :], Qs[n][:, :].rearrange("p (b n) -> p b n", b=8), jm[:, j:j + 1], None, ALU.mult),
                            [r, *last.get(("Qblk", p), ())], sig="b_qb")
                h["Q", g_] = k
                last["Qs", n] = (k,)

            def vproj():
                i, bk, fr = PS.get()
                for t in range(4):
                    m = add("pe", lambda e, t=t: e.matmul(bk[:, t * 128:t * 128 + 128], cxT[p][:, t * 128:t * 128 + 128], xWv[:, :], start=True, stop=True),
                            [got["cxT", s], *fr], sig="b_v")
                last["cxT", p] = (m,)
                b3 = bk[:, :].rearrange("p (n c) -> p n c", c=8)
                add("act", lambda e: e.activation(V4[p][0:64, :, 0:8], b3[0:64], ACT.Copy), [m, vset, *last.get(("V", p), ())], sig="b_ve")
                h["V"] = add("act", lambda e: e.activation(V4[p][64:128, :, 9:17], b3[64:128], ACT.Copy), (), sig="b_ve")
                PS.free(i, h["V"])

            def score(b):
                i, bk, fr = PS.get()
                for g_ in range(4):
                    for jj in range(2):
                        m = add("pe", lambda e, g_=g_, jj=jj: e.matmul(
                            bk[:, (4 * jj + g_) * 64:(4 * jj + g_) * 64 + 64], Q5[p][:, g_, b, 2 * jj:2 * jj + 2, :],
                            Ks[p][:, g_ * 512 + b * 64:g_ * 512 + b * 64 + 64], start=True, stop=True),
                            [h["Q", g_], h["K", g_], *fr], sig="b_s" if (g_, jj) == (3, 1) else None)
                h["mx", b] = add("dve", lambda e: e.tensor_reduce(mx[p][:, b:64:8], bk[:, :].rearrange("p (n k) -> p n k", k=64), AX.X, ALU.max),
                                 [m, *last.get(("mx", p), ())], sig="b_mx")
                PS.free(i, h["mx", b])

            order = [(0.9, kproj), (0.9, vproj), (1.50, None)]
            order += [(0.45, lambda g_=g_: kspread(g_)) for g_ in range(4)]
            order += [(0.45, flip), (1.33, None), (0.9, qproj), (1.50, None)]
            order += [(0.45, lambda g_=g_: qspread(g_)) for g_ in range(4)]
            order += [(0.80, None)] + [(0.3, lambda b=b: score(b)) for b in range(8)] + [(1.00, None)]
            return order

        def stage_b2(s):
            p = s % 2
            h = hb.setdefault(s, {})

            def rows():
                i, bk, fr = PS.get()
                m = add("pe", lambda e: e.transpose(bk[0:64, 0:128], mx[p][:, :], ident[:, :]), [h["mx", 7], *fr], sig="b_mT")
                last["mx", p] = (m,)
                r = add("act", lambda e: e.activation(Mrow[p][:, :], bk[0:64, 0:128], ACT.Copy, scale=-1.0 / 128), [m, *last.get(("M", p), ())], sig="b_M")
                PS.free(i, r)
                for j in range(4):
                    r0 = 32 * (j // 2)
                    h["M"] = add("sp", lambda e, j=j, r0=r0: e.dma_start(
                        Qblk[p][32 * j + 24:32 * j + 25, :].rearrange("p (m j n) -> p m j n", j=4, n=64)[:, :, j, :],
                        Mrow[p][r0:r0 + 32, 64 * (j % 2):64 * (j % 2) + 64]), [r], sig=f"dma_M{p}", inc=16)
                last["M", p] = (h["M"],)

            def prob(t, hf):
                n = t % 2
                i, bk, fr = PS.get()
                for gg in range(2):
                    g_ = 2 * hf + gg
                    for bb in range(2):
                        b = 2 * t + bb
                        o = bk[64 * bb:64 * bb + 64, gg * 256:gg * 256 + 256]
                        m = add("pe", lambda e, o=o, g_=g_, b=b: e.matmul(o, Ks[p][:, g_ * 512 + b * 64:g_ * 512 + b * 64 + 64], Q5[p][:, g_, b, :, :], start=True, stop=True),
                                [h["M"], vset, *fr], sig="b_st" if (gg, bb) == (1, 1) else None)
                if (t, hf) == (3, 1):
                    last["Qblk", p] = last["Ks", p] = (m,)
                h["P", t, hf] = add("act", lambda e: e.activation(PT[n][:, hf * 512:hf * 512 + 512], bk[:, :], ACT.Exp, scale=SM), [m, *last.get(("PT", n), ())], sig="b_exp")
                PS.free(i, h["P", t, hf])

            def pv(t):
                n = t % 2
                i, bk, fr = PS.get()
                for hh in range(H):
                    g_, j = hh // 4, hh % 4
                    m = add("pe", lambda e, hh=hh, g_=g_, j=j: e.matmul(bk[32 * j:32 * j + 32, g_ * 64:g_ * 64 + 64], V4[p][:, t * 16 + hh, :], PT[n][:, hh * 64:hh * 64 + 64],
                                                                    start=True, stop=True), [h["P", t, 0], h["P", t, 1], h["V"], *fr] if hh == 0 else (), sig="b_pv" if hh == 15 else None)
                last["PT", n] = (m,)
                if t == 3:
                    last["V", p] = (m,)
                h["O", t] = add("dve", lambda e: e.tensor_copy(OT[n][:, :], bk[:, 0:256]), [m, *last.get(("OT", n), ())], sig="b_oe")
                PS.free(i, h["O", t])

            def unflip(t):
                n = t % 2
                i, bk, fr = PS.get()
                for g_ in range(4):
                    m = add("pe", lambda e, g_=g_: e.transpose(bk[0:64, g_ * 128:g_ * 128 + 128], OT[n][:, g_ * 64:g_ * 64 + 64], ident[:, :]), [h["O", t], *fr], sig="b_tr")
                last["OT", n] = (m,)
                b3 = bk[0:64, :].rearrange("p (h c) -> p h c", c=32)
                r3_ = rs[n][:, :].rearrange("p (h c) -> p h c", c=2)
                d = add("dve", lambda e: e.reciprocal(r3_, b3[:, :, 8:18:9]), [m, *last.get(("rs", n), ())], sig="b_rs")
                for bb in range(2):
                    c = add("dve", lambda e, bb=bb: e.tensor_tensor(cn[n][:, bb * 128:bb * 128 + 128].rearrange("p (h c) -> p h c", c=8), b3[:, :, 9 * bb:9 * bb + 8],
                                                              r3_[:, :, bb:bb + 1].to_broadcast([64, 16, 8]), ALU.mult), [d, *last.get(("cn", n), ())], sig="b_cn")
                last["rs", n] = (c,)
                h["c", t] = c
                PS.free(i, c)

            def reflip(t):
                n = t % 2
                i, bk, fr = PS.get()
                for bb in range(2):
                    m = add("pe", lambda e, bb=bb: e.transpose(bk[:, bb * 64:bb * 64 + 64], cn[n][:, bb * 128:bb * 128 + 128], ident[0:64, 0:64]), [h["c", t], *fr], sig="b_tr2")
                last["cn", n] = (m,)
                h["cT", t] = add("act", lambda e: e.activation(cT[n][:, :], bk[:, 0:128], ACT.Copy), [m, *last.get(("cT", n), ())], sig="b_cT")
                PS.free(i, h["cT", t])

            def outp(t):
                n = t % 2
                i, bk, fr = PS.get()
                m = add("pe", lambda e: e.matmul(bk[:, 0:128], cT[n][:, :], xWo[:, :], start=True, stop=True), [h["cT", t], *fr], sig="b_o")
                last["cT", n] = (m,)
                h["r", t] = add("dve", lambda e: e.tensor_tensor(x2[p][:, t * 128:t * 128 + 128], bk[:, 0:128], x1b[s % 3][:, t * 128:t * 128 + 128], ALU.add),
                                [m, got["x1b", s], *last.get(("x2", p), ())], sig="b_r")
                PS.free(i, h["r", t])
                if t == 3:
                    last["x1b", s % 3] = (h["r", 3],)

            def norm():
                x = layernorm("2", x2[p], [h["r", t] for t in range(4)])
                got["x2", s] = x
                got["x2b", s] = add("pool", lambda e: e.tensor_tensor(x2b[p][:, :].rearrange("p (t d) -> p t d", t=4), x2[p][:, :].rearrange("p (t d) -> p t d", t=4),
                                                                    bias3[:, :].unsqueeze(1).to_broadcast([128, 4, 128]), ALU.add),
                                    [x[-1], *last.get(("x2b", p), ())], sig="b_x2b")

            order = [(0.1, rows), (1.20, None)]
            order += [(0.6, lambda t=t, hf=hf: prob(t, hf)) for t in range(2) for hf in range(2)]
            for t in range(4):
                order.append((0.75, lambda t=t: pv(t)))
                if t < 2:
                    order.append((0.6, lambda t=t: prob(t + 2, 0)))
                if t:
                    order.append((0.25, lambda t=t: unflip(t - 1)))
                if t < 2:
                    order.append((0.6, lambda t=t: prob(t + 2, 1)))
                if t > 1:
                    order.append((0.15, lambda t=t: reflip(t - 2)))
                    order.append((0.25, lambda t=t: outp(t - 2)))
            order += [(0.70, None), (0.25, lambda: unflip(3)), (0.15, lambda: reflip(2)), (1.04, None), (0.25, lambda: outp(2)),
                      (0.15, lambda: reflip(3)), (0.46, None), (0.25, lambda: outp(3)), (0.5, norm)]
            return order

        def stage_c(s):
            p = s % 2
            h = {}
            st, mv, ve, rstd = stats["4"]

            def flip():
                i, bk, fr = PS.get()
                for t in range(4):
                    m = add("pe", lambda e, t=t: e.transpose(bk[:, t * 128:t * 128 + 128], x2[p][:, t * 128:t * 128 + 128], ident[:, :]), [got["x2", s][t], *fr], sig="b_xT")
                last["x2", p] = (m, got["x2b", s])
                hi = add("act", lambda e: e.activation(x2h[:, :], bk[:, :], ACT.Copy), [m, *last.get("x2T", ())], sig="b_x2h")
                got["x2T", s] = add("dve", lambda e: e.tensor_tensor(x2l[:, :], bk[:, :], x2h[:, :], ALU.subtract), [hi, *last.get("x2T", ())], sig="b_x2l")
                PS.free(i, got["x2T", s])

            def up():
                for t in range(4):
                    i, bk, fr = PS.get()
                    sl = slice(t * 128, t * 128 + 128)
                    add("pe", lambda e, bk=bk, sl=sl: e.matmul(bk[:, :], x2h[:, sl], tfc[:, :], start=True, stop=False), [got["x2T", s], *fr])
                    m = add("pe", lambda e, bk=bk, sl=sl: e.matmul(bk[:, :], x2l[:, sl], tfc[:, :], start=False, stop=True), (), sig="c_up")
                    h["g", t] = add("act", lambda e, bk=bk, t=t: e.activation(g[t][:, :], bk[:, :], ACT.Gelu), [m, *last.get(("g", t), ())], sig="c_g")
                    PS.free(i, h["g", t])
                last["x2T"] = (m,)

            def stat():
                for t in range(4):
                    b = add("dve", lambda e, t=t: e.bn_stats(st[:, 6 * t:6 * t + 6], g[t][:, :]), [h["g", t], *last.get("st4", ())], sig="c_st")
                for t in range(4):
                    m = add("dve", lambda e, t=t: e.bn_aggr(mv[:, 2 * t:2 * t + 2], st[:, 6 * t:6 * t + 6]), [b], sig="c_mv")
                h["mv"] = m
                v = add("pool", lambda e: e.tensor_scalar(ve[:, :], mv[:, 1::2], 1e-5, 1.0, ALU.add, ALU.mult), [m, *last.get("st4", ())], sig="c_ve")
                h["rstd"] = add("pool", lambda e: e.tensor_tensor(rstd[:, :], ve[:, :], mhalf[:, :], ALU.pow), [v, o2], sig="c_rstd")

            def centre(t):
                n = t % 2
                d = add("dve", lambda e: e.scalar_tensor_tensor(g[t][:, :], g[t][:, :], mv[:, 2 * t:2 * t + 1], lnw[:, :], ALU.subtract, ALU.mult),
                        [h["mv"], *prepared], sig="c_gn")
                d = add("act", lambda e: e.activation(gh[n][:, 0:512], g[t][:, :], ACT.Copy), [d, *last.get(("gh", n), ())], sig="c_gh")
                h["gn", t] = add("pool", lambda e: e.tensor_tensor(gh[n][:, 512:1024], g[t][:, :], gh[n][:, 0:512], ALU.subtract), [d, *last.get(("gh", n), ())], sig="c_gl")
                last["g", t] = (h["gn", t],)

            def turn(t):
                n = t % 2
                i, bk, fr = PS.get()
                b16 = bk[:, :].bitcast(F16)
                for c in range(8):
                    m = add("pe", lambda e, c=c: e.transpose(b16[:, c * 128:c * 128 + 128], gh[n][:, c * 128:c * 128 + 128], identh[:, :]), [h["gn", t], *fr], sig="c_tr")
                last["gh", n] = (m,)
                h["gT", t] = add("act", lambda e: e.activation(gT[n][:, :], b16, ACT.Copy), [m, *last.get(("gT", n), ())], sig="c_gT")
                PS.free(i, h["gT", t])

            def down(t):
                n = t % 2
                i, bk, fr = PS.get()
                for c in range(8):
                    m = add("pe", lambda e, c=c: e.matmul(bk[:, 0:128], gT[n][:, c * 128:c * 128 + 128], tpj[:, c % 4 * 128:c % 4 * 128 + 128], start=(c == 0), stop=(c == 7)),
                            [h["gT", t], *fr] if c == 0 else (), sig="c_dn" if c == 7 else None)
                last["gT", n] = (m,)
                h["r", t] = add("dve", lambda e: e.scalar_tensor_tensor(yo[p][:, t * 128:t * 128 + 128], bk[:, 0:128], rstd[:, t:t + 1], x2b[p][:, t * 128:t * 128 + 128], ALU.mult, ALU.add),
                                [m, h["rstd"], got["x2b", s], *last.get(("yo", p), ())], sig="c_r")
                PS.free(i, h["r", t])
                if t == 3:
                    last["x2b", p] = last["st4"] = (h["r", 3],)

            def norm():
                x = layernorm("3", yo[p], [h["r", t] for t in range(4)])
                got["y", s] = add("sp", lambda e: e.dma_start(out[s], yo[p][:, :]), [x[-1]], sig=f"dma_y{p}", inc=16)
                last["yo", p] = (got["y", s],)

            order = [(0.5, flip), (0.80, None), (1.9, up), (1.00, None), (0.1, stat), (0.50, None),
                     (0.1, lambda: centre(0)), (0.90, None), (0.1, lambda: centre(1)), (0.90, None),
                     (0.5, lambda: turn(0)), (0.1, lambda: centre(2)), (0.90, None), (0.6, lambda: down(0)),
                     (0.5, lambda: turn(1)), (0.1, lambda: centre(3)), (0.90, None), (0.6, lambda: down(1)),
                     (0.5, lambda: turn(2)), (0.90, None), (0.6, lambda: down(2)), (0.5, lambda: turn(3)), (0.90, None),
                     (0.6, lambda: down(3)), (0.5, norm)]
            return order

        loads_x(0)
        loads_x(1)
        loads_c(0)
        split_x(0)
        PHASE = {"a": 0.0, "b1": 0.76, "b2": 1.75, "c": 2.87}
        order = []

        def place_part(start, n, part):
            whole, before = sum(c for c, _ in part), 0.0
            for k, (c, f) in enumerate(part):
                if f is not None:
                    order.append((start + (before + c / 2) / whole, n, k, f))
                before += c

        for s in range(NG):
            place_part(s + PHASE["c"], 0, stage_c(s))
            place_part(s + PHASE["b2"], 1, stage_b2(s))
            place_part(s + PHASE["b1"], 2, stage_b1(s))
            place_part(s + PHASE["a"], 3, stage_a(s))
            if s + 1 < NG:
                place_part(s + 0.08, 4, [(0.1, lambda s=s: split_x(s + 1)), (1.00, None)])
            if 0 < s < NG - 1:
                place_part(s + 0.05, 5, [(0.1, lambda s=s: loads_x(s + 1)), (1.00, None)])
            if s > 0:
                place_part(s + 0.05, 5, [(0.1, lambda s=s: loads_c(s)), (0.35, None)])
        for _, _, _, f in sorted(order, key=lambda o: o[:3]):
            f()
        add("sp", lambda e: e.nop(), [got["y", NG - 2], got["y", NG - 1]])

        block = ctx.enter_context(nc.Block())

        @block.sync
        def _(e):
            q.emit("sp", e)

        @block.gpsimd
        def _(e):
            q.emit("pool", e)

        @block.scalar
        def _(e):
            q.emit("act", e)

        @block.vector
        def _(e):
            q.emit("dve", e)

        @block.tensor
        def _(e):
            q.emit("pe", e)


def constants():
    f = np.float32
    p = np.arange(128)
    c = {}
    c["ident"] = np.eye(128, dtype=f)
    c["ones2"] = (p[:, None] // 64 == p[None, :] // 64).astype(f)
    c["jm"] = (p[:, None] // 32 == np.arange(4)[None, :]).astype(f)
    c["tmask"] = np.where(p[:, None] // 16 == np.arange(4)[None, :], f(-1e-6), f(0))
    e = np.arange(128)
    for k, high in (("q", (0, 2)), ("k", (0, 1))):
        for part, reps in (("h", high), ("l", (3 - sum(high),))):
            m = np.zeros((128, 4, 4, 4, 8), np.float16)
            for rep in reps:
                m[e, e // 32, e // 8 % 4, rep, e % 8] = 1
            c["place_" + k + part] = m.reshape(128, 512)
    c["kone"] = np.where(p % 32 == 24, f(128), f(0))[:, None]
    return c


def kernel(**inputs):
    import concourse.bacc as bacc
    from concourse.bass_utils import run_bass_kernel_spmd as run

    w = {k: np.asarray(v) for k, v in inputs.items()}
    f = np.float32
    A = {}
    A["x_nat"] = w["x"].reshape(NG, 4, 128, D).transpose(0, 2, 1, 3).reshape(NG, 128, 512)
    A["xT"] = w["x"].reshape(NG, 512, D).transpose(0, 2, 1)
    A["cxT"] = w["ctx_1024"].reshape(NG, 512, D).transpose(0, 2, 1)

    def pairs(W):
        return W.reshape(8, 128, -1).transpose(1, 0, 2).reshape(128, -1)

    for k in "qkv":
        A[f"W{k}T"] = pairs(w[f"L0_attn_W{k}"].T)
    for k in "qk":
        m = np.zeros((128, 64), f)
        m[0:64, 0:32] = w[f"L0_attn_w{k}_feat"]
        m[64:128, 32:64] = w[f"L0_attn_w{k}_feat"]
        A[f"feat{k}"] = m
        A[f"b{k}T"] = w[f"L0_attn_b{k}"].reshape(8, 128).T
    A["Wpj"] = pairs(w["L0_attn_Wproj"])
    bv = w["L0_attn_bv"].reshape(8, 2, 64)
    blk = np.zeros((2, 64, 8, 8, 16), f)
    for c in range(8):
        for hp in range(2):
            blk[hp, :, c, :, 2 * c + hp] = bv[c, hp][:, None]
    A["bvblk"] = blk.reshape(128, 1024)
    A["bvrep"] = np.repeat(w["L0_attn_bv"].reshape(8, 128).T[:, :, None], 128, axis=2).reshape(128, 1024)
    A["bproj"] = w["L0_attn_bproj"].reshape(1, 128)
    A["bo"] = w["L0_xattn_bo"].reshape(1, 128)
    for k in "qk":
        A[f"xW{k}"] = w[f"L0_xattn_W{k}"].T
        A[f"xb{k}"] = w[f"L0_xattn_b{k}"].reshape(128, 1)
    A["xWv"] = w["L0_xattn_Wv"].T
    A["xWo"] = w["L0_xattn_Wo"].T
    A["xbvrep"] = np.repeat(w["L0_xattn_bv"][:, None], 128, axis=1)
    A["Wfc"] = w["L0_ffn_W_fc"].T
    A["Wpr"] = w["L0_ffn_W_proj"].T.reshape(4, 128, 128).transpose(1, 0, 2).reshape(128, 512)
    A["lnw"] = np.repeat(w["L0_ffn_ln_w"][None, :], 128, axis=0)
    A["lnbrep"] = np.repeat(w["L0_ffn_ln_b"].reshape(4, 128).T[:, :, None], 128, axis=2).reshape(128, 512)
    A.update(constants())

    nc = bacc.Bacc("TRN2", target_bir_lowering=False, num_devices=1)
    arrays, aps = {}, {}
    for name, v in A.items():
        v = np.ascontiguousarray(v)
        arrays["in_" + name] = v
        aps[name] = nc.dram_tensor("in_" + name, v.shape, mybir.dt.from_np(v.dtype), kind="ExternalInput").ap()
    o = nc.dram_tensor("out_y", (NG, 128, 512), mybir.dt.float32, kind="ExternalOutput").ap()
    decoder_kernel(nc, aps, o)
    r = run(nc, [arrays], core_ids=[0])
    y = np.asarray(r.results[0]["out_y"])
    return y.reshape(NG, 128, 4, D).transpose(0, 2, 1, 3).reshape(NB, T, D)
```

```python
import numpy as np
import concourse.bass as bass
from concourse import mybir
from contextlib import ExitStack

NB = 128
T = 64
D = 128
NG = 16
H = 16


class Queues:

    def __init__(self, nc, ctx):
        self.nc, self.ctx = nc, ctx
        self.sems, self.count = {}, {}
        self.lists = {e: [] for e in ("pe", "act", "dve", "pool", "sp")}

    def add(self, eng, fn, waits=(), sig=None, inc=1):
        done = None
        if sig is not None:
            if sig not in self.sems:
                self.sems[sig] = self.ctx.enter_context(self.nc.semaphore("s_" + sig))
                self.count[sig] = 0
            self.count[sig] += inc
            done = (sig, self.count[sig])
        self.lists[eng].append((fn, tuple(w for w in waits if w is not None), sig, inc))
        return done

    def emit(self, eng, e):
        seen = {}
        for fn, waits, sig, inc in self.lists[eng]:
            need = {}
            for name, value in waits:
                need[name] = max(need.get(name, 0), value)
            for name, value in need.items():
                if seen.get(name, 0) < value:
                    e.wait_ge(self.sems[name], value)
                    seen[name] = value
            ins = fn(e)
            if sig is not None:
                ins.then_inc(self.sems[sig], inc)


class Banks:

    def __init__(self, banks):
        self.banks, self.freed, self.n = banks, [()] * len(banks), 0

    def get(self):
        i = self.n % len(self.banks)
        self.n += 1
        return i, self.banks[i], self.freed[i]

    def free(self, i, *reads):
        self.freed[i] = reads


SMALL1 = (0, 64, 128, 136, 144, 272)
SMALL2 = (0, 128, 640, 768, 896, 1024, 1152, 1280, 1281, 1282, 1286, 1290, 1291)


def decoder_kernel(nc, a, out):
    F32, F16, BF = mybir.dt.float32, mybir.dt.float16, mybir.dt.bfloat16
    ALU, ACT, AX = mybir.AluOpType, mybir.ActivationFunctionType, mybir.AxisListType
    SM = 8.0 ** -0.5

    with ExitStack() as ctx:
        q = Queues(nc, ctx)
        add = q.add

        def sb(name, cols, dt=F32, parts=128):
            return ctx.enter_context(nc.sbuf_tensor(name, [parts, cols], dt))

        banks = [ctx.enter_context(nc.psum_tensor(f"bank{i}", [128, 512], F32)) for i in range(8)]
        PS = Banks(banks)

        two = range(2)
        Qblk, PT, kp = [sb(f"Qblk{i}", 8192, F16) for i in two], [sb(f"PT{i}", 1024) for i in two], sb("kp", 2048)
        late = [Qblk[n][:, 2048 * i:2048 * i + 2048].bitcast(F32) for n in two for i in range(4)]
        both = Qblk[0][:, :].bitcast(F32)

        def load(name, t, sig):
            add("sp", lambda e: e.dma_start(t, a[name]), sig=sig, inc=16)

        xs, xT, cxT = [sb(f"xs{i}", 512) for i in two], sb("xT", 512), [sb(f"cxT{i}", 512) for i in two]
        small1, small2, row1 = sb("small1", SMALL1[-1]), sb("small2", SMALL2[-1]), sb("row1", 256, F32, 1)
        load("small1", small1[:, :], "w_first")
        load("WqkT", both[:, 0:2048], "w_first")
        got = {("xT", 0): add("sp", lambda e: e.dma_start(xT[:, :], a["xT"][0]), (), sig="dma_xT", inc=16)}
        load("Wvp", both[:, 2048:4096], "w_rest")
        load("small2", small2[:, :], "w_rest")
        load("Wff", Qblk[1][:, 0:3072].bitcast(F32), "w_rest")
        load("bvblk", PT[0][:, :], "w_rest")
        load("bvrep", PT[1][:, :], "w_rest")
        load("row1", row1[:, :], "w_rest")
        first, weights = ("w_first", 32), ("w_rest", 96)
        WqT, WkT, WvT, Wpj = late[0:4]
        Wfc, Wpr, lnb = late[4][:, 0:512], late[4][:, 512:1024], late[5][:, 0:512]
        tmp, tpr, brow = late[5][:, 512:1024], late[6][:, 0:512], [late[6][0:1, 512:1024], late[7][0:1, 0:512], late[7][0:1, 512:1024]]
        bvblk, bvrep = PT
        bpj, bo = row1[0:1, 0:128], row1[0:1, 128:256]
        fq, fk, bqT, bkT, ones2 = [small1[:, SMALL1[i]:SMALL1[i + 1]] for i in range(5)]
        ident, lnw, xWq, xWk, xWv, xWo, xbv, xbq, xbk, jm, tmask, kone = [small2[:, SMALL2[i]:SMALL2[i + 1]] for i in range(12)]

        ones = sb("ones", 128)
        mhalf = sb("mhalf", 4)
        o1 = add("dve", lambda e: e.memset(ones[:, :], 1.0), sig="const")
        o2 = add("dve", lambda e: e.memset(mhalf[:, :], -0.5), sig="const")

        Mh = sb("Mh", 2048)
        Wqf, Wkf = [(sb(f"W{k}fh", 512, F16), sb(f"W{k}fl", 512, F16)) for k in "qk"]
        onesb, qbias = sb("onesb", 128, BF), sb("qbias", 512, BF)
        nbeta, biasA, bias2, bias3 = sb("nbeta", 512), sb("biasA", 128), sb("bias2", 128), sb("bias3", 128)
        tfc, tpj, identh = sb("tfc", 512, F16), sb("tpj", 512, F16), sb("identh", 128, F16)
        o3 = add("dve", lambda e: e.memset(onesb[:, :], 1.0), sig="const")
        o4 = add("dve", lambda e: e.memset(qbias[:, :], 0.0), sig="const")

        def pe(fns, waits, sig="w_pe"):
            for f in fns[:-1]:
                add("pe", f, waits)
                waits = ()
            return add("pe", fns[-1], waits, sig=sig)

        def prep1():
            ready = [o3]
            for W, f, dst in ((WqT, fq, Wqf), (WkT, fk, Wkf)):
                i, bk, fr = PS.get()
                m = pe([lambda e, W=W, f=f, bk=bk, c=c: e.matmul(bk[:, c * 64:c * 64 + 64], W[:, c * 128:c * 128 + 128], f[:, :], start=True, stop=True)
                        for c in range(8)], [first, *fr])
                r = add("act", lambda e, bk=bk, dst=dst: e.activation(dst[0][:, :], bk[:, :], ACT.Copy), [m], sig="w_act")
                r = add("dve", lambda e, bk=bk, dst=dst: e.tensor_tensor(dst[1][:, :], bk[:, :], dst[0][:, :], ALU.subtract), [r], sig="w_dve")
                PS.free(i, r)
                ready.append(r)
            i, bk, fr = PS.get()
            fns = []
            for c in range(8):
                o = bk[0:1, c * 64:c * 64 + 64]
                fns.append(lambda e, o=o, c=c: e.matmul(o, bqT[:, c:c + 1], fq[:, :], start=True, stop=False))
                fns.append(lambda e, o=o, c=c: e.matmul(o, bkT[:, c:c + 1], fk[:, :], start=False, stop=True))
            m = pe(fns, fr)
            rest = [bk[0:1, :], brow[0], brow[1]]
            r = o4
            for n in range(3):
                o = qbias[32 * n:32 * n + 1, :]
                r = add("dve", lambda e, n=n, o=o: e.tensor_copy(o, rest[n]), [m, r], sig="w_dve")
                if n < 2:
                    r = add("dve", lambda e, n=n, o=o: e.tensor_copy(brow[2], o), [r], sig="w_dve")
                    r = add("dve", lambda e, n=n, o=o: e.tensor_tensor(rest[n + 1], rest[n], brow[2], ALU.subtract), [r], sig="w_dve")
            PS.free(i, r)
            ready.append(r)
            return ready

        def prep2():
            ready = []
            for c in range(4):
                i, bk, fr = PS.get()
                fns = []
                hp, r0 = c % 2, 64 * (c % 2)
                for k in range(4):
                    w = slice((4 * (c // 2) + k) * 128, (4 * (c // 2) + k) * 128 + 128)
                    fns.append(lambda e, bk=bk, k=k, w=w, r0=r0: e.matmul(
                        bk[:, k * 128:k * 128 + 128], WvT[r0:r0 + 64, w], Wpj[r0:r0 + 64, w], start=True, stop=True))
                m = pe(fns, [weights, *fr])
                o = Mh[:, :].rearrange("p (c k a n) -> p c k a n", c=2, k=4, a=2)[:, c // 2, :, hp, :]
                r = add("act", lambda e, bk=bk, o=o: e.activation(o, bk[:, :].rearrange("p (k n) -> p k n", k=4), ACT.Copy), [m], sig="w_act")
                PS.free(i, r)
                ready.append(r)

            def acc(lhs, rhs, row, n):
                fns = [lambda e, c=c, bk=bk: e.matmul(bk[:, 0:128], lhs[:, c * 128:c * 128 + 128], rhs[:, c * 128:c * 128 + 128],
                                                      start=(c == 0), stop=(c == n - 1 and row is None)) for c in range(n)]
                if row is not None:
                    fns.append(lambda e, bk=bk: e.matmul(bk[:, 0:128], ones[0:1, 0:128], row[0:1, :], start=False, stop=True))
                return fns

            for lhs, rhs, row, n, dst, scale in ((bvrep, Wpj, bpj, 8, biasA, 1.0),
                                                 (xbv, xWo, bo, 1, bias2, 1.0)):
                i, bk, fr = PS.get()
                m = pe(acc(lhs, rhs, row, n), [o1, *fr])
                r = add("act", lambda e, bk=bk, dst=dst, scale=scale: e.activation(dst[:, :], bk[:, 0:128], ACT.Copy, scale=scale), [m], sig="w_act")
                PS.free(i, r)
                ready.append(r)
            i, bk, fr = PS.get()
            m = pe(acc(bvblk, Wpj, None, 8), fr)
            for t in range(4):
                r = add("act", lambda e, bk=bk, t=t: e.activation(nbeta[:, t * 128:t * 128 + 128], bk[:, 0:128], ACT.Copy, scale=tmask[:, t:t + 1]), [m], sig="w_act")
            PS.free(i, r)
            ready.append(r)
            colsum, hg = sb("colsum", 2), sb("hg", 4)
            for n, W in enumerate((Wfc, Wpr)):
                c = add("dve", lambda e, n=n, W=W: e.tensor_reduce(colsum[:, n:n + 1], W[:, :], AX.X, ALU.add, apply_absolute_value=True),
                        [weights], sig="w_dve")
            i, bk, fr = PS.get()
            m = pe([lambda e, bk=bk: e.matmul(bk[:, 0:2], ones[:, :], colsum[:, :], start=True, stop=True)], [c, *fr])
            h1 = add("dve", lambda e, bk=bk: e.tensor_scalar(hg[:, 0:2], bk[:, 0:2], 1.0 / 65536, 1e-6, ALU.mult, ALU.add), [m], sig="w_dve")
            PS.free(i, h1)
            h2 = add("dve", lambda e: e.tensor_scalar(hg[:, 2:4], hg[:, 0:2], -0.5, None, ALU.mult), [h1], sig="w_dve")
            h3 = add("dve", lambda e: e.tensor_scalar(hg[:, 0:2], hg[:, 0:2], 0.5, None, ALU.mult), [h2], sig="w_dve")
            for n, (W, dst) in enumerate(((Wfc, tfc), (Wpr, tpr))):
                t1 = add("dve", lambda e, n=n, W=W: e.tensor_scalar(tmp[:, :], W[:, :], hg[:, 2 + n:3 + n], None, ALU.is_lt), [h3], sig="w_dve")
                h3 = add("dve", lambda e, n=n, W=W, dst=dst: e.scalar_tensor_tensor(dst[:, :], W[:, :], hg[:, n:n + 1], tmp[:, :], ALU.is_gt, ALU.subtract),
                         [t1], sig="w_dve")
            ready.append(add("dve", lambda e: e.tensor_copy(tpj[:, :], tpr[:, :]), [h3], sig="w_dve"))
            ready.append(add("dve", lambda e: e.tensor_copy(identh[:, :], ident[:, :]), [h3], sig="w_dve"))
            i, bk, fr = PS.get()
            m = pe(acc(lnb, tpr, None, 4), [h3, *fr])
            r = add("act", lambda e, bk=bk: e.activation(bias3[:, :], bk[:, 0:128], ACT.Copy), [m], sig="w_act")
            PS.free(i, r)
            ready.append(r)
            return ready

        prepared1 = prep1()
        prepared = list(prepared1)

        xh, xl = [sb(f"xh{i}", 512, F16) for i in two], [sb(f"xl{i}", 512, F16) for i in two]
        qn, prod, qT = [sb(f"qn{i}", 512) for i in range(4)], sb("prod", 512), sb("qT", 2048)
        dsum, Dv, DT, xb = sb("dsum", 64), sb("Dv", 128), sb("DT", 128), sb("xb", 512)
        GT, Cb = [sb(f"GT{i}", 512) for i in range(3)], [sb(f"Cb{i}", 512) for i in range(4)]
        x1, x1b, x1T = [sb(f"x1{i}", 512) for i in two], [sb(f"x1b{i}", 512) for i in range(3)], sb("x1T", 512)
        Qh, Ql = [sb(f"Qh{i}", 512, F16) for i in two], [sb(f"Ql{i}", 512, F16) for i in two]
        Qs, Ks = sb("Qs", 2048, F16), [sb(f"Ks{i}", 2048, F16) for i in two]
        Vblk = [sb(f"Vblk{i}", 2048) for i in two]
        mx, Mrow = [sb(f"mx{i}", 64) for i in two], [sb(f"Mrow{i}", 128, F16, 64) for i in two]
        OT = [sb(f"OT{i}", 256) for i in two]
        rs, cn, cT = [sb(f"rs{i}", 32, F32, 64) for i in two], [sb(f"cn{i}", 256, F32, 64) for i in two], [sb(f"cT{i}", 128) for i in two]
        x2, x2b = [sb(f"x2{i}", 512) for i in two], [sb(f"x2b{i}", 512) for i in two]
        x2h, x2l = sb("x2h", 512, F16), sb("x2l", 512, F16)
        g, gT = [sb(f"g{i}", 512) for i in range(4)], [sb(f"gT{i}", 1024, F16) for i in two]
        gh = [sb(f"gh{i}", 1024, F16) for i in two]
        yo = [sb(f"yo{i}", 512) for i in two]
        stats = {k: (sb("st" + k, 24), sb("mv" + k, 8), sb("ve" + k, 4), sb("rstd" + k, 4)) for k in "1234"}

        V4 = [v[:, :].rearrange("p (n c) -> p n c", c=32) for v in Vblk]
        o5 = add("dve", lambda e: e.memset(Dv[:, :], 0.0), sig="const")
        vset = []

        def set_zeros():
            v = None
            for n in two:
                v = add("pool", lambda e, n=n: e.memset(Vblk[n][:, :], 0.0), [v], sig="const_pool")
                v = add("pool", lambda e, n=n: e.memset(V4[n][0:64, :, 8:9], 1.0), [v], sig="const_pool")
                v = add("pool", lambda e, n=n: e.memset(V4[n][64:128, :, 17:18], 1.0), [v], sig="const_pool")
                v = add("pool", lambda e, n=n: e.memset(Ks[n][:, :], 0.0), [v], sig="const_pool")
                v = add("pool", lambda e, n=n: e.tensor_scalar(Ks[n][:, :], Ks[n][:, :], kone[:, 0:1], 1.0, ALU.add, ALU.mult), [v, weights], sig="const_pool")
            v = add("pool", lambda e: e.memset(Qs[:, :], 0.0), [v], sig="const_pool")
            vset.append(v)

        last = {(k, n): prepared for k in ("Qblk", "PT") for n in two}

        def loads_x(s):
            p = s % 2
            got["xs", s] = add("sp", lambda e: e.dma_start(xs[p][:, :], a["x_nat"][s]), last.get(("xs", p), ()), sig=f"dma_xs{p}", inc=16)
            if s > 0:
                got["xT", s] = add("sp", lambda e: e.dma_start(xT[:, :], a["xT"][s]), last.get("xT", ()), sig="dma_xT", inc=16)

        def split_x(s):
            p = s % 2
            hi = add("pool", lambda e: e.tensor_copy(xh[p][:, :], xT[:, :]), [got["xT", s], *last.get(("xhl", p), ())], sig="a_xh")
            got["xhl", s] = add("pool", lambda e: e.tensor_tensor(xl[p][:, :], xT[:, :], xh[p][:, :], ALU.subtract), [hi], sig="a_xl")
            last["xT"] = (got["xhl", s],)

        def loads_c(s):
            p = s % 2
            got["cxT", s] = add("sp", lambda e: e.dma_start(cxT[p][:, :], a["cxT"][s]), last.get(("cxT", p), ()), sig=f"dma_cx{p}", inc=16)

        def layernorm(k, x, summed, eps=1e-5):
            st, mv, ve, rstd = stats[k]
            for t in range(4):
                b = add("dve", lambda e, t=t: e.bn_stats(st[:, 6 * t:6 * t + 6], x[:, t * 128:t * 128 + 128]), [summed[t], *last.get(("st", k), ())], sig="ln_st" + k)
            for t in range(4):
                m = add("dve", lambda e, t=t: e.bn_aggr(mv[:, 2 * t:2 * t + 2], st[:, 6 * t:6 * t + 6]), [b, *last.get(("st", k), ())], sig="ln_mv" + k)
            v = add("pool", lambda e: e.tensor_scalar(ve[:, :], mv[:, 1::2], eps, 1.0, ALU.add, ALU.mult), [m], sig="ln_ve" + k)
            r = add("pool", lambda e: e.tensor_tensor(rstd[:, :], ve[:, :], mhalf[:, :], ALU.pow), [v, o2], sig="ln_r" + k)
            done = []
            for t in range(4):
                done.append(add("dve", lambda e, t=t: e.tensor_scalar(
                    x[:, t * 128:t * 128 + 128], x[:, t * 128:t * 128 + 128], mv[:, 2 * t:2 * t + 1], rstd[:, t:t + 1], ALU.subtract, ALU.mult),
                    [r, m], sig="ln_x" + k))
            last["st", k] = (done[-1],)
            return done

        def stage_a(s):
            p = s % 2
            h = {}

            def logits(bk, t, W, stop, waits, sig):
                sl = slice(t * 128, t * 128 + 128)
                add("pe", lambda e: e.matmul(bk[:, :], xh[p][:, sl], W[0][:, :], start=True, stop=False), waits)
                add("pe", lambda e: e.matmul(bk[:, :], xh[p][:, sl], W[1][:, :], start=False, stop=False))
                return add("pe", lambda e: e.matmul(bk[:, :], xl[p][:, sl], W[0][:, :], start=False, stop=stop), (), sig=sig)

            def kexp(t):
                i, bk, fr = PS.get()
                m = logits(bk, t, Wkf, True, [got["xhl", s], *prepared1[1:3], *fr], "a_k")
                h["k", t] = add("act", lambda e: e.activation(kp[:, t * 512:t * 512 + 512], bk[:, :], ACT.Exp),
                                [m, *last.get("kp", ())], sig="a_kexp")
                PS.free(i, h["k", t])

            def qexp(t):
                n = t
                i, bk, fr = PS.get()
                logits(bk, t, Wqf, False, [got["xhl", s], *fr], None)
                m = add("pe", lambda e: e.matmul(bk[:, :], onesb[:, :], qbias[:, :], start=False, stop=True), prepared1, sig="a_q")
                if t == 3:
                    last["xhl", p] = (m,)
                h["q", t] = add("act", lambda e: e.activation(qn[n][:, :], bk[:, :], ACT.Exp), [m, *last.get(("qn", n), ())], sig="a_qexp")
                PS.free(i, h["q", t])

            def ksum(t):
                n = t
                i, bk, fr = PS.get()
                m = add("pe", lambda e: e.matmul(bk[:, :], ones2[:, :], kp[:, t * 512:t * 512 + 512], start=True, stop=True), [h["k", t], *fr], sig="a_ks")
                d = add("dve", lambda e: e.tensor_tensor(prod[:, :], qn[n][:, :], bk[:, :], ALU.mult), [m, h["q", t], *last.get("prod", ())], sig="a_pr")
                PS.free(i, d)
                d = add("dve", lambda e: e.tensor_reduce(dsum[:, t * 16:t * 16 + 16], prod[:, :].rearrange("p (h f) -> p h f", f=32), AX.X, ALU.add), [d], sig="a_ds")
                last["prod"] = (d,)
                d = add("dve", lambda e: e.tensor_scalar(dsum[:, t * 16:t * 16 + 16], dsum[:, t * 16:t * 16 + 16], 1e-6, None, ALU.add), [d], sig="a_ds")
                h["D", t] = add("dve", lambda e: e.reciprocal(Dv[:, t * 16:t * 16 + 16], dsum[:, t * 16:t * 16 + 16]), [d, o5, *last.get("Dv", ())], sig="a_dv")
                v = qn[n][:, :].rearrange("p (h f) -> p h f", f=32)
                h["qn", t] = add("pool", lambda e: e.tensor_tensor(v, v, Dv[:, t * 16:t * 16 + 16].unsqueeze(2).to_broadcast([128, 16, 32]), ALU.mult), [h["D", t]], sig="a_qn")

            def qturn(t):
                n = t
                i, bk, fr = PS.get()
                for g_ in range(4):
                    m = add("pe", lambda e, g_=g_: e.transpose(bk[:, g_ * 128:g_ * 128 + 128], qn[n][:, g_ * 128:g_ * 128 + 128], ident[:, :]),
                            [h["qn", t], *fr], sig="a_qT")
                last["qn", n] = (m,)
                o = qT[:, :].rearrange("p (g n) -> p g n", g=4)[:, :, t * 128:t * 128 + 128]
                h["qT", t] = add("act", lambda e: e.activation(o, bk[:, :].rearrange("p (g n) -> p g n", g=4), ACT.Copy), [m, *last.get("qT", ())], sig="a_qTe")
                PS.free(i, h["qT", t])

            def dturn():
                i, bk, fr = PS.get()
                m = add("pe", lambda e: e.transpose(bk[:, 0:128], Dv[:, :], ident[:, :]), [h["D", 3], *fr], sig="a_DT")
                last["Dv"] = (m, h["qn", 3])
                h["DT"] = add("act", lambda e: e.activation(DT[:, :], bk[:, 0:128], ACT.Copy), [m, *last.get("DT", ())], sig="a_DTe")
                PS.free(i, h["DT"])

            def gmat(b):
                t, r0 = b // 2, 64 * (b % 2)
                i, bk, fr = PS.get()
                m = add("pe", lambda e: e.matmul(bk[:, :], xs[p][r0:r0 + 64, t * 128:t * 128 + 128], kp[r0:r0 + 64, t * 512:t * 512 + 512], start=True, stop=True),
                        [got["xs", s], h["k", t], *fr], sig="a_g")
                if b == 7:
                    last["kp"] = (m,)
                    h["gend"] = m
                n = b % 3
                eng, f = (("act", lambda e: e.activation(GT[n][:, :], bk[:, :], ACT.Copy)) if b % 2 else ("dve", lambda e: e.tensor_copy(GT[n][:, :], bk[:, :])))
                h["G", b] = add(eng, f, [m, *last.get(("GT", n), ())], sig="a_ge_" + eng)
                PS.free(i, h["G", b])

            def cmat(b):
                i, bk, fr = PS.get()
                n, n4 = b % 3, b % 4
                for hh in range(H):
                    g_, j = hh // 4, hh % 4
                    m = add("pe", lambda e, hh=hh, g_=g_, j=j: e.matmul(
                        bk[32 * j:32 * j + 32, g_ * 128:g_ * 128 + 128], GT[n][:, hh * 32:hh * 32 + 32], Mh[:, hh * 128:hh * 128 + 128], start=True, stop=True),
                        [h["G", b], *fr] if hh == 0 else (), sig="a_c" if hh == 15 else None)
                last["GT", n] = (m,)
                eng, f = (("dve", lambda e: e.tensor_copy(Cb[n4][:, :], bk[:, :])) if b % 2 else ("act", lambda e: e.activation(Cb[n4][:, :], bk[:, :], ACT.Copy)))
                h["C", b] = add(eng, f, [m, *last.get(("Cb", n4), ())], sig="a_ce_" + eng)
                PS.free(i, h["C", b])

            def outp(t):
                i, bk, fr = PS.get()
                for bb in range(2):
                    add("pe", lambda e, bb=bb: e.matmul(bk[64 * bb:64 * bb + 64, 0:128], DT[:, 64 * bb:64 * bb + 64], nbeta[:, t * 128:t * 128 + 128], start=True, stop=False),
                        [h["DT"], *fr])
                for g_ in range(4):
                    for bb in range(2):
                        b = 2 * t + bb
                        m = add("pe", lambda e, g_=g_, bb=bb, b=b: e.matmul(
                            bk[64 * bb:64 * bb + 64, 0:128], qT[:, g_ * 512 + b * 64:g_ * 512 + b * 64 + 64], Cb[b % 4][:, g_ * 128:g_ * 128 + 128],
                            start=False, stop=(g_ == 3)), [h["C", b], h["qT", t]], sig="a_o" if (g_, bb) == (3, 1) else None)
                for bb in range(2):
                    last["Cb", (2 * t + bb) % 4] = (m,)
                if t == 3:
                    last["qT"] = last["DT"] = (m,)
                h["r", t] = add("dve", lambda e: e.tensor_tensor(x1[p][:, t * 128:t * 128 + 128], bk[:, 0:128], xb[:, t * 128:t * 128 + 128], ALU.add),
                                [m, h["xb"], *last.get(("x1", p), ())], sig="a_r")
                PS.free(i, h["r", t])

            def xbias():
                o = xb[:, :].rearrange("p (t d) -> p t d", t=4)
                h["xb"] = add("pool", lambda e: e.tensor_tensor(o, xs[p][:, :].rearrange("p (t d) -> p t d", t=4), biasA[:, :].unsqueeze(1).to_broadcast([128, 4, 128]), ALU.add),
                              [got["xs", s], *prepared, *last.get("xb", ())], sig="a_xb")

            def norm():
                last["xb"] = (h["r", 3],)
                last["xs", p] = (h["gend"], h["xb"])
                x = layernorm("1", x1[p], [h["r", t] for t in range(4)])
                got["x1", s] = x
                n = s % 3
                got["x1b", s] = add("pool", lambda e: e.tensor_tensor(x1b[n][:, :].rearrange("p (t d) -> p t d", t=4), x1[p][:, :].rearrange("p (t d) -> p t d", t=4),
                                                                    bias2[:, :].unsqueeze(1).to_broadcast([128, 4, 128]), ALU.add),
                                    [x[-1], *last.get(("x1b", n), ())], sig="a_x1b")

            order = []
            for step in "k0 k1 k2 k3 q0 D0 g0 q1 D1 xb g1 c0 q2 D2 g2 c1 q3 D3 g3 c2 r0 g4 r1 c3 dt r2 g5 o0 c4 r3 g6 c5 o1 g7 c6 o2 c7 .. o3".split():
                if step == "..":
                    order.append((1.20, None))
                elif step == "xb":
                    order.append((0.1, xbias))
                elif step == "dt":
                    order.append((0.1, dturn))
                else:
                    fn, cost = {"k": (kexp, 0.7), "q": (qexp, 0.9), "D": (ksum, 0.9), "g": (gmat, 0.9), "c": (cmat, 1.2), "r": (qturn, 0.5), "o": (outp, 1.2)}[step[0]]
                    order.append((cost, lambda fn=fn, n=int(step[1]): fn(n)))
            order.append((0.5, norm))
            return order

        hb = {}
        Q5 = [t[:, :].rearrange("p (g b j n) -> p g b j n", g=4, b=8, j=4) for t in Qblk]

        def stage_b1(s):
            p = s % 2
            h = hb.setdefault(s, {})

            def flip():
                i, bk, fr = PS.get()
                for t in range(4):
                    m = add("pe", lambda e, t=t: e.transpose(bk[:, t * 128:t * 128 + 128], x1[p][:, t * 128:t * 128 + 128], ident[:, :]), [got["x1", s][t], *fr], sig="a_xT")
                last["x1", p] = (m, got["x1b", s])
                h["x1T"] = add("act", lambda e: e.activation(x1T[:, :], bk[:, :], ACT.Copy), [m, *last.get("x1T", ())], sig="a_x1T")
                PS.free(i, h["x1T"])

            def proj(k, W, src, ready, bias):
                n = "qk".index(k)
                i, bk, fr = PS.get()
                m = add("pe", lambda e: e.matmul(bk[:, :], W[:, :], src[:, :], start=True, stop=True), [ready, *fr], sig="b_p")
                free = last.get(("Qh", n), ())
                hi = add("act", lambda e: e.activation(Qh[n][:, :], bk[:, :], ACT.Identity, bias=bias[:, 0:1]), [m, *free], sig="b_hi")
                h["hi" + k] = hi
                h["lo" + k] = add("dve", lambda e: e.scalar_tensor_tensor(Ql[n][:, :], bk[:, :], bias[:, 0:1], Qh[n][:, :], ALU.add, ALU.subtract), [hi, *free], sig="b_lo")
                PS.free(i, h["lo" + k])
                return m

            def spread(k, out, parts, free):
                n = "qk".index(k)
                for j in range(4):
                    for rep, part in enumerate(parts):
                        r0 = 32 * j + 8 * rep
                        src = (Qh, Ql)[part][n]
                        d = add("sp", lambda e, j=j, r0=r0, src=src: e.dma_start(out[r0:r0 + 8, :].rearrange("p (g n) -> p g n", g=4), src[32 * j:32 * j + 32, :]),
                                [h["hi" + k], h["lo" + k], *vset, *free], sig=f"dma_{k}{p}", inc=16)
                last["Qh", n] = (d,)
                return d

            def kproj():
                proj("k", xWk, cxT[p], got["cxT", s], xbk)

            def qproj():
                last["x1T"] = (proj("q", xWq, x1T, h["x1T"], xbq),)

            def kspread():
                h["K"] = spread("k", Ks[p], (0, 0, 1), last.get(("Ks", p), ()))

            def qspread():
                h["Qs"] = spread("q", Qs, (0, 1, 0), last.get("Qs", ()))

            def qblock(j):
                h["Q"] = add("dve", lambda e: e.tensor_scalar(Qblk[p][:, :].rearrange("p (m j n) -> p m j n", j=4, n=64)[:, :, j, :],
                                                           Qs[:, :].rearrange("p (m n) -> p m n", n=64), jm[:, j:j + 1], None, ALU.mult),
                             [h["Qs"], *last.get(("Qblk", p), ())], sig="b_qb")
                last["Qs"] = (h["Q"],)

            def vproj():
                i, bk, fr = PS.get()
                for t in range(4):
                    m = add("pe", lambda e, t=t: e.matmul(bk[:, t * 128:t * 128 + 128], cxT[p][:, t * 128:t * 128 + 128], xWv[:, :], start=True, stop=True),
                            [got["cxT", s], *fr], sig="b_v")
                last["cxT", p] = (m,)
                b3 = bk[:, :].rearrange("p (n c) -> p n c", c=8)
                add("act", lambda e: e.activation(V4[p][0:64, :, 0:8], b3[0:64], ACT.Copy), [m, *vset, *last.get(("V", p), ())], sig="b_ve")
                h["V"] = add("act", lambda e: e.activation(V4[p][64:128, :, 9:17], b3[64:128], ACT.Copy), (), sig="b_ve")
                PS.free(i, h["V"])

            def score(b):
                i, bk, fr = PS.get()
                for g_ in range(4):
                    for jj in range(2):
                        m = add("pe", lambda e, g_=g_, jj=jj: e.matmul(
                            bk[:, (4 * jj + g_) * 64:(4 * jj + g_) * 64 + 64], Q5[p][:, g_, b, 2 * jj:2 * jj + 2, :],
                            Ks[p][:, g_ * 512 + b * 64:g_ * 512 + b * 64 + 64], start=True, stop=True),
                            [h["Q"], h["K"], *fr], sig="b_s" if (g_, jj) == (3, 1) else None)
                h["mx", b] = add("dve", lambda e: e.tensor_reduce(mx[p][:, b:64:8], bk[:, :].rearrange("p (n k) -> p n k", k=64), AX.X, ALU.max),
                                 [m, *last.get(("mx", p), ())], sig="b_mx")
                PS.free(i, h["mx", b])

            order = [(0.9, kproj), (0.9, vproj), (0.50, None), (0.1, kspread), (1.35, None),
                     (0.45, flip), (1.33, None), (0.9, qproj), (1.50, None), (0.1, qspread), (3.00, None)]
            order += [(0.2, lambda j=j: qblock(j)) for j in range(4)]
            order += [(1.50, None)] + [(0.3, lambda b=b: score(b)) for b in range(8)] + [(1.00, None)]
            return order

        def stage_b2(s):
            p = s % 2
            h = hb.setdefault(s, {})

            def rows():
                i, bk, fr = PS.get()
                m = add("pe", lambda e: e.transpose(bk[0:64, 0:128], mx[p][:, :], ident[:, :]), [h["mx", 7], *fr], sig="b_mT")
                last["mx", p] = (m,)
                r = add("act", lambda e: e.activation(Mrow[p][:, :], bk[0:64, 0:128], ACT.Copy, scale=-1.0 / 128), [m, *last.get(("M", p), ())], sig="b_M")
                PS.free(i, r)
                for j in range(4):
                    r0 = 32 * (j // 2)
                    h["M"] = add("sp", lambda e, j=j, r0=r0: e.dma_start(
                        Qblk[p][32 * j + 24:32 * j + 25, :].rearrange("p (m j n) -> p m j n", j=4, n=64)[:, :, j, :],
                        Mrow[p][r0:r0 + 32, 64 * (j % 2):64 * (j % 2) + 64]), [r], sig=f"dma_M{p}", inc=16)
                last["M", p] = (h["M"],)

            def prob(t, hf):
                n = t % 2
                i, bk, fr = PS.get()
                for gg in range(2):
                    g_ = 2 * hf + gg
                    for bb in range(2):
                        b = 2 * t + bb
                        o = bk[64 * bb:64 * bb + 64, gg * 256:gg * 256 + 256]
                        m = add("pe", lambda e, o=o, g_=g_, b=b: e.matmul(o, Ks[p][:, g_ * 512 + b * 64:g_ * 512 + b * 64 + 64], Q5[p][:, g_, b, :, :], start=True, stop=True),
                                [h["M"], *vset, *fr], sig="b_st" if (gg, bb) == (1, 1) else None)
                if (t, hf) == (3, 1):
                    last["Qblk", p] = last["Ks", p] = (m,)
                h["P", t, hf] = add("act", lambda e: e.activation(PT[n][:, hf * 512:hf * 512 + 512], bk[:, :], ACT.Exp, scale=SM), [m, *last.get(("PT", n), ())], sig="b_exp")
                PS.free(i, h["P", t, hf])

            def pv(t):
                n = t % 2
                i, bk, fr = PS.get()
                for hh in range(H):
                    g_, j = hh // 4, hh % 4
                    m = add("pe", lambda e, hh=hh, g_=g_, j=j: e.matmul(bk[32 * j:32 * j + 32, g_ * 64:g_ * 64 + 64], V4[p][:, t * 16 + hh, :], PT[n][:, hh * 64:hh * 64 + 64],
                                                                    start=True, stop=True), [h["P", t, 0], h["P", t, 1], h["V"], *fr] if hh == 0 else (), sig="b_pv" if hh == 15 else None)
                last["PT", n] = (m,)
                if t == 3:
                    last["V", p] = (m,)
                h["O", t] = add("dve", lambda e: e.tensor_copy(OT[n][:, :], bk[:, 0:256]), [m, *last.get(("OT", n), ())], sig="b_oe")
                PS.free(i, h["O", t])

            def unflip(t):
                n = t % 2
                i, bk, fr = PS.get()
                for g_ in range(4):
                    m = add("pe", lambda e, g_=g_: e.transpose(bk[0:64, g_ * 128:g_ * 128 + 128], OT[n][:, g_ * 64:g_ * 64 + 64], ident[:, :]), [h["O", t], *fr], sig="b_tr")
                last["OT", n] = (m,)
                b3 = bk[0:64, :].rearrange("p (h c) -> p h c", c=32)
                r3_ = rs[n][:, :].rearrange("p (h c) -> p h c", c=2)
                d = add("dve", lambda e: e.reciprocal(r3_, b3[:, :, 8:18:9]), [m, *last.get(("rs", n), ())], sig="b_rs")
                for bb in range(2):
                    c = add("dve", lambda e, bb=bb: e.tensor_tensor(cn[n][:, bb * 128:bb * 128 + 128].rearrange("p (h c) -> p h c", c=8), b3[:, :, 9 * bb:9 * bb + 8],
                                                              r3_[:, :, bb:bb + 1].to_broadcast([64, 16, 8]), ALU.mult), [d, *last.get(("cn", n), ())], sig="b_cn")
                last["rs", n] = (c,)
                h["c", t] = c
                PS.free(i, c)

            def reflip(t):
                n = t % 2
                i, bk, fr = PS.get()
                for bb in range(2):
                    m = add("pe", lambda e, bb=bb: e.transpose(bk[:, bb * 64:bb * 64 + 64], cn[n][:, bb * 128:bb * 128 + 128], ident[0:64, 0:64]), [h["c", t], *fr], sig="b_tr2")
                last["cn", n] = (m,)
                h["cT", t] = add("act", lambda e: e.activation(cT[n][:, :], bk[:, 0:128], ACT.Copy), [m, *last.get(("cT", n), ())], sig="b_cT")
                PS.free(i, h["cT", t])

            def outp(t):
                n = t % 2
                i, bk, fr = PS.get()
                m = add("pe", lambda e: e.matmul(bk[:, 0:128], cT[n][:, :], xWo[:, :], start=True, stop=True), [h["cT", t], *fr], sig="b_o")
                last["cT", n] = (m,)
                h["r", t] = add("dve", lambda e: e.tensor_tensor(x2[p][:, t * 128:t * 128 + 128], bk[:, 0:128], x1b[s % 3][:, t * 128:t * 128 + 128], ALU.add),
                                [m, got["x1b", s], *last.get(("x2", p), ())], sig="b_r")
                PS.free(i, h["r", t])
                if t == 3:
                    last["x1b", s % 3] = (h["r", 3],)

            def norm():
                x = layernorm("2", x2[p], [h["r", t] for t in range(4)])
                got["x2", s] = x
                got["x2b", s] = add("pool", lambda e: e.tensor_tensor(x2b[p][:, :].rearrange("p (t d) -> p t d", t=4), x2[p][:, :].rearrange("p (t d) -> p t d", t=4),
                                                                    bias3[:, :].unsqueeze(1).to_broadcast([128, 4, 128]), ALU.add),
                                    [x[-1], *last.get(("x2b", p), ())], sig="b_x2b")

            order = [(0.1, rows), (2.69, None)]
            order += [(0.4, lambda t=t, hf=hf: prob(t, hf)) for t in range(2) for hf in range(2)]
            for t in range(7):
                if t < 4:
                    order.append((0.75, lambda t=t: pv(t)))
                if 0 <= t - 3:
                    order.append((0.25, lambda t=t: outp(t - 3)))
                if t < 2:
                    order.append((0.4, lambda t=t: prob(t + 2, 0)))
                if 0 <= t - 1 < 4:
                    order.append((0.4, lambda t=t: unflip(t - 1)))
                if t < 2:
                    order.append((0.4, lambda t=t: prob(t + 2, 1)))
                if 0 <= t - 2 < 4:
                    order.append((0.15, lambda t=t: reflip(t - 2)))
                if t > 1:
                    order.append((0.60, None))
            order.append((0.5, norm))
            return order

        def stage_c(s):
            p = s % 2
            h = {}
            st, mv, ve, rstd = stats["4"]

            def flip():
                i, bk, fr = PS.get()
                for t in range(4):
                    m = add("pe", lambda e, t=t: e.transpose(bk[:, t * 128:t * 128 + 128], x2[p][:, t * 128:t * 128 + 128], ident[:, :]), [got["x2", s][t], *fr], sig="b_xT")
                last["x2", p] = (m, got["x2b", s])
                hi = add("act", lambda e: e.activation(x2h[:, :], bk[:, :], ACT.Copy), [m, *last.get("x2T", ())], sig="b_x2h")
                got["x2T", s] = add("dve", lambda e: e.tensor_tensor(x2l[:, :], bk[:, :], x2h[:, :], ALU.subtract), [hi, *last.get("x2T", ())], sig="b_x2l")
                PS.free(i, got["x2T", s])

            def up():
                for t in range(4):
                    i, bk, fr = PS.get()
                    sl = slice(t * 128, t * 128 + 128)
                    add("pe", lambda e, bk=bk, sl=sl: e.matmul(bk[:, :], x2h[:, sl], tfc[:, :], start=True, stop=False), [got["x2T", s], *fr])
                    m = add("pe", lambda e, bk=bk, sl=sl: e.matmul(bk[:, :], x2l[:, sl], tfc[:, :], start=False, stop=True), (), sig="c_up")
                    h["g", t] = add("act", lambda e, bk=bk, t=t: e.activation(g[t][:, :], bk[:, :], ACT.Gelu), [m, *last.get(("g", t), ())], sig="c_g")
                    PS.free(i, h["g", t])
                last["x2T"] = (m,)

            def stat():
                for t in range(4):
                    b = add("dve", lambda e, t=t: e.bn_stats(st[:, 6 * t:6 * t + 6], g[t][:, :]), [h["g", t], *last.get("st4", ())], sig="c_st")
                for t in range(4):
                    m = add("dve", lambda e, t=t: e.bn_aggr(mv[:, 2 * t:2 * t + 2], st[:, 6 * t:6 * t + 6]), [b], sig="c_mv")
                h["mv"] = m
                v = add("pool", lambda e: e.tensor_scalar(ve[:, :], mv[:, 1::2], 1e-5, 1.0, ALU.add, ALU.mult), [m, *last.get("st4", ())], sig="c_ve")
                h["rstd"] = add("pool", lambda e: e.tensor_tensor(rstd[:, :], ve[:, :], mhalf[:, :], ALU.pow), [v, o2], sig="c_rstd")

            def centre(t):
                n = t % 2
                d = add("dve", lambda e: e.scalar_tensor_tensor(g[t][:, :], g[t][:, :], mv[:, 2 * t:2 * t + 1], lnw[:, :], ALU.subtract, ALU.mult),
                        [h["mv"], *prepared], sig="c_gn")
                d = add("act", lambda e: e.activation(gh[n][:, 0:512], g[t][:, :], ACT.Copy), [d, *last.get(("gh", n), ())], sig="c_gh")
                h["gn", t] = add("pool", lambda e: e.tensor_tensor(gh[n][:, 512:1024], g[t][:, :], gh[n][:, 0:512], ALU.subtract), [d, *last.get(("gh", n), ())], sig="c_gl")
                last["g", t] = (h["gn", t],)

            def turn(t):
                n = t % 2
                i, bk, fr = PS.get()
                b16 = bk[:, :].bitcast(F16)
                for c in range(8):
                    m = add("pe", lambda e, c=c: e.transpose(b16[:, c * 128:c * 128 + 128], gh[n][:, c * 128:c * 128 + 128], identh[:, :]), [h["gn", t], *fr], sig="c_tr")
                last["gh", n] = (m,)
                h["gT", t] = add("act", lambda e: e.activation(gT[n][:, :], b16, ACT.Copy), [m, *last.get(("gT", n), ())], sig="c_gT")
                PS.free(i, h["gT", t])

            def down(t):
                n = t % 2
                i, bk, fr = PS.get()
                for c in range(8):
                    m = add("pe", lambda e, c=c: e.matmul(bk[:, 0:128], gT[n][:, c * 128:c * 128 + 128], tpj[:, c % 4 * 128:c % 4 * 128 + 128], start=(c == 0), stop=(c == 7)),
                            [h["gT", t], *fr] if c == 0 else (), sig="c_dn" if c == 7 else None)
                last["gT", n] = (m,)
                h["r", t] = add("dve", lambda e: e.scalar_tensor_tensor(yo[p][:, t * 128:t * 128 + 128], bk[:, 0:128], rstd[:, t:t + 1], x2b[p][:, t * 128:t * 128 + 128], ALU.mult, ALU.add),
                                [m, h["rstd"], got["x2b", s], *last.get(("yo", p), ())], sig="c_r")
                PS.free(i, h["r", t])
                if t == 3:
                    last["x2b", p] = last["st4"] = (h["r", 3],)

            def norm():
                x = layernorm("3", yo[p], [h["r", t] for t in range(4)])
                got["y", s] = add("sp", lambda e: e.dma_start(out[s], yo[p][:, :]), [x[-1]], sig=f"dma_y{p}", inc=16)
                last["yo", p] = (got["y", s],)

            order = [(0.5, flip), (0.80, None), (1.9, up), (1.00, None), (0.1, stat), (0.37, None),
                     (0.1, lambda: centre(0)), (0.90, None), (0.1, lambda: centre(1)), (0.90, None),
                     (0.5, lambda: turn(0)), (0.1, lambda: centre(2)), (0.90, None), (0.6, lambda: down(0)),
                     (0.5, lambda: turn(1)), (0.1, lambda: centre(3)), (0.72, None), (0.6, lambda: down(1)),
                     (0.5, lambda: turn(2)), (0.90, None), (0.6, lambda: down(2)), (0.5, lambda: turn(3)), (0.90, None),
                     (0.6, lambda: down(3)), (0.5, norm)]
            return order

        loads_x(0)
        loads_c(0)
        split_x(0)
        set_zeros()
        loads_x(1)
        PHASE = {"a": 0.0, "b1": 0.87, "b2": 1.82, "c": 2.94}
        order = []

        def place_part(start, n, part):
            whole, before = sum(c for c, _ in part), 0.0
            for k, (c, f) in enumerate(part):
                if f is not None:
                    order.append((start + (before + c / 2) / whole, n, k, f))
                before += c

        for s in range(NG):
            place_part(s + PHASE["c"], 0, stage_c(s))
            place_part(s + PHASE["b2"], 1, stage_b2(s))
            place_part(s + PHASE["b1"], 2, stage_b1(s))
            place_part(s + PHASE["a"], 3, stage_a(s))
            if s == 0:
                place_part(0.1, 6, [(1.0, lambda: prepared.extend(prep2())), (9.00, None)])
            if s + 1 < NG:
                place_part(s + 0.08, 4, [(0.1, lambda s=s: split_x(s + 1)), (1.00, None)])
            if 0 < s < NG - 1:
                place_part(s + 0.05, 5, [(0.1, lambda s=s: loads_x(s + 1)), (1.00, None)])
            if s > 0:
                place_part(s + 0.05, 5, [(0.1, lambda s=s: loads_c(s)), (0.23, None)])
        for _, _, _, f in sorted(order, key=lambda o: o[:3]):
            f()
        add("sp", lambda e: e.nop(), [got["y", NG - 2], got["y", NG - 1]])

        block = ctx.enter_context(nc.Block())

        @block.sync
        def _(e):
            q.emit("sp", e)

        @block.gpsimd
        def _(e):
            q.emit("pool", e)

        @block.scalar
        def _(e):
            q.emit("act", e)

        @block.vector
        def _(e):
            q.emit("dve", e)

        @block.tensor
        def _(e):
            q.emit("pe", e)


def constants():
    f = np.float32
    p = np.arange(128)
    c = {}
    c["ident"] = np.eye(128, dtype=f)
    c["ones2"] = (p[:, None] // 64 == p[None, :] // 64).astype(f)
    c["jm"] = (p[:, None] // 32 == np.arange(4)[None, :]).astype(f)
    c["tmask"] = np.where(p[:, None] // 16 == np.arange(4)[None, :], f(-1e-6), f(0))
    c["kone"] = np.where(p % 32 == 24, f(128), f(0))[:, None]
    return c


def kernel(**inputs):
    import concourse.bacc as bacc
    from concourse.bass_utils import run_bass_kernel_spmd as run

    w = {k: np.asarray(v) for k, v in inputs.items()}
    f = np.float32
    A = {}
    A["x_nat"] = w["x"].reshape(NG, 4, 128, D).transpose(0, 2, 1, 3).reshape(NG, 128, 512)
    A["xT"] = w["x"].reshape(NG, 512, D).transpose(0, 2, 1)
    A["cxT"] = w["ctx_1024"].reshape(NG, 512, D).transpose(0, 2, 1)

    def pairs(W):
        return W.reshape(8, 128, -1).transpose(1, 0, 2).reshape(128, -1)

    c = constants()
    WT = {k: pairs(w[f"L0_attn_W{k}"].T) for k in "qkv"}
    feat = {}
    for k in "qk":
        feat[k] = np.zeros((128, 64), f)
        feat[k][0:64, 0:32] = feat[k][64:128, 32:64] = w[f"L0_attn_w{k}_feat"]
    A["small1"] = np.concatenate([feat["q"], feat["k"], *[w[f"L0_attn_b{k}"].reshape(8, 128).T for k in "qk"], c["ones2"]], axis=1)
    A["WqkT"] = np.concatenate([WT["q"], WT["k"]], axis=1)
    A["Wvp"] = np.concatenate([WT["v"], pairs(w["L0_attn_Wproj"])], axis=1)
    bv = w["L0_attn_bv"].reshape(8, 2, 64)
    blk = np.zeros((2, 64, 8, 8, 16), f)
    for i in range(8):
        for hp in range(2):
            blk[hp, :, i, :, 2 * i + hp] = bv[i, hp][:, None]
    A["bvblk"] = blk.reshape(128, 1024)
    A["bvrep"] = np.repeat(w["L0_attn_bv"].reshape(8, 128).T[:, :, None], 128, axis=2).reshape(128, 1024)
    A["row1"] = np.concatenate([w["L0_attn_bproj"], w["L0_xattn_bo"]])[None, :]
    xW = [w[f"L0_xattn_W{k}"].T.reshape(128, 4, 4, 8).transpose(0, 2, 3, 1).reshape(128, 128) for k in "qk"]
    xb = [w[f"L0_xattn_b{k}"].reshape(4, 4, 8).transpose(1, 2, 0).reshape(128, 1) for k in "qk"]
    A["small2"] = np.concatenate([
        c["ident"], np.repeat(w["L0_ffn_ln_w"][None, :], 128, axis=0), *xW, w["L0_xattn_Wv"].T, w["L0_xattn_Wo"].T,
        np.repeat(w["L0_xattn_bv"][:, None], 128, axis=1), *xb, c["jm"], c["tmask"], c["kone"]], axis=1)
    A["Wff"] = np.concatenate([w["L0_ffn_W_fc"].T, w["L0_ffn_W_proj"].T.reshape(4, 128, 128).transpose(1, 0, 2).reshape(128, 512),
                               np.repeat(w["L0_ffn_ln_b"].reshape(4, 128).T[:, :, None], 128, axis=2).reshape(128, 512)], axis=1)

    nc = bacc.Bacc("TRN2", target_bir_lowering=False, num_devices=1)
    arrays, aps = {}, {}
    for name, v in A.items():
        v = np.ascontiguousarray(v)
        arrays["in_" + name] = v
        aps[name] = nc.dram_tensor("in_" + name, v.shape, mybir.dt.from_np(v.dtype), kind="ExternalInput").ap()
    o = nc.dram_tensor("out_y", (NG, 128, 512), mybir.dt.float32, kind="ExternalOutput").ap()
    decoder_kernel(nc, aps, o)
    r = run(nc, [arrays], core_ids=[0])
    y = np.asarray(r.results[0]["out_y"])
    return y.reshape(NG, 128, 4, D).transpose(0, 2, 1, 3).reshape(NB, T, D)
```
